# Optimizing a Trainium2 kernel written in Bass

```python
import numpy as np
import jax
import jax.numpy as jnp

def _softmax(x, axis=-1):
    return jax.nn.softmax(x, axis=axis)

def _gelu(x):
    return jax.nn.gelu(x, approximate=True)

def _silu(x):
    return jax.nn.silu(x)

def _sigmoid(x):
    return jax.nn.sigmoid(x)

def _layernorm(x, axis=-1, eps=1e-05):
    m = jnp.mean(x, axis=axis, keepdims=True)
    v = jnp.var(x, axis=axis, keepdims=True)
    return (x - m) / jnp.sqrt(v + eps)

def _scatter_add(tgt, idx, src, axis=0):
    return tgt.at[idx].add(src)

def _segment_sum(src, seg, n):
    return jax.ops.segment_sum(src, seg, n)
kernel_name = 'mk_xattn_seq_d1_seqx_r4_e9e1e8'

def setup_inputs(seed: int=0):
    np.random.seed(seed)
    _w = jnp.asarray

    def _rec_inputs():
        import jax
        import jax.numpy as jnp
        _rk = jax.random.key(seed)
        x = -0.0002928 + 1 * jax.random.normal(jax.random.fold_in(_rk, 1), (4, 1024, 256), jnp.float32)
        _lenS = 1024 - jax.random.randint(jax.random.fold_in(_rk, 7), (4,), 0, max(1, 1024 // 4) + 1, jnp.int32)
        _lenS2 = 77 - jax.random.randint(jax.random.fold_in(_rk, 8), (4,), 0, max(1, 77 // 4) + 1, jnp.int32)
        _ctx_1024P = jax.random.normal(jax.random.fold_in(_rk, 11), (4, 16, 256), jnp.float32)
        _ctx_1024c = jax.random.dirichlet(jax.random.fold_in(_rk, 511), 0.3 * jnp.ones((16,), jnp.float32), (4, 77))
        _ctx_1024t = jnp.einsum('bsk,bkd->bsd', _ctx_1024c, _ctx_1024P)
        _ctx_1024t = _ctx_1024t * jax.lax.rsqrt(jnp.mean(jnp.square(_ctx_1024t)) + 1e-12) * 0.953939
        ctx_1024 = -1.39393e-06 + 0.999914 * (_ctx_1024t + 0.3 * jax.random.normal(jax.random.fold_in(_rk, 611), (4, 77, 256), jnp.float32))
        return (x, ctx_1024)
    x, ctx_1024 = _rec_inputs()

    def _L0_xattn_setup():
        import jax, jax.numpy as jnp
        import numpy as np
        D = 256
        H = 16
        HD = D // H
        DFF = 4 * D
        LN_EPS = 1e-05

        def layernorm(x, gamma, beta):
            mu = jnp.mean(x, axis=-1, keepdims=True)
            var = jnp.mean(jnp.square(x - mu), axis=-1, keepdims=True)
            return (x - mu) * jax.lax.rsqrt(var + LN_EPS) * gamma + beta
        key = jax.random.key(seed)
        ks = jax.random.split(key, 10)
        B, Nq, Nk = (2, 512, 512)
        s = 0.02
        return {'q_x': jax.random.normal(ks[0], (B, Nq, D), jnp.float32), 'kv_x': jax.random.normal(ks[1], (B, Nk, D), jnp.float32), 'Wq': jax.random.normal(ks[2], (D, D), jnp.float32) * s, 'Wkv': jax.random.normal(ks[3], (2 * D, D), jnp.float32) * s, 'Wo': jax.random.normal(ks[4], (D, D), jnp.float32) * s, 'bo': jnp.zeros((D,), jnp.float32), 'ln_q_g': jnp.ones((D,), jnp.float32), 'ln_q_b': jnp.zeros((D,), jnp.float32), 'ln_kv_g': jnp.ones((D,), jnp.float32), 'ln_kv_b': jnp.zeros((D,), jnp.float32), 'W1': jax.random.normal(ks[5], (DFF, D), jnp.float32) * s, 'b1': jnp.zeros((DFF,), jnp.float32), 'W2': jax.random.normal(ks[6], (D, DFF), jnp.float32) * s, 'b2': jnp.zeros((D,), jnp.float32)}
    _L0_xattn_all = _L0_xattn_setup()
    _L0_xattn_in = {k: v for k, v in _L0_xattn_all.items() if k in ('Wq', 'Wkv', 'Wo', 'bo', 'ln_q_g', 'ln_q_b', 'ln_kv_g', 'ln_kv_b', 'W1', 'b1', 'W2', 'b2')}
    del _L0_xattn_all
    return {'x': x, 'ctx_1024': ctx_1024, 'L0_xattn_Wq': _L0_xattn_in['Wq'], 'L0_xattn_Wkv': _L0_xattn_in['Wkv'], 'L0_xattn_Wo': _L0_xattn_in['Wo'], 'L0_xattn_bo': _L0_xattn_in['bo'], 'L0_xattn_ln_q_g': _L0_xattn_in['ln_q_g'], 'L0_xattn_ln_q_b': _L0_xattn_in['ln_q_b'], 'L0_xattn_ln_kv_g': _L0_xattn_in['ln_kv_g'], 'L0_xattn_ln_kv_b': _L0_xattn_in['ln_kv_b'], 'L0_xattn_W1': _L0_xattn_in['W1'], 'L0_xattn_b1': _L0_xattn_in['b1'], 'L0_xattn_W2': _L0_xattn_in['W2'], 'L0_xattn_b2': _L0_xattn_in['b2']}

def reference(x, ctx_1024, L0_xattn_Wq, L0_xattn_Wkv, L0_xattn_Wo, L0_xattn_bo, L0_xattn_ln_q_g, L0_xattn_ln_q_b, L0_xattn_ln_kv_g, L0_xattn_ln_kv_b, L0_xattn_W1, L0_xattn_b1, L0_xattn_W2, L0_xattn_b2):
    import jax
    import jax.numpy as jnp

    def _L0_xattn_ref(q_x, kv_x, Wq, Wkv, Wo, bo, ln_q_g, ln_q_b, ln_kv_g, ln_kv_b, W1, b1, W2, b2):
        import jax, jax.numpy as jnp
        import numpy as np
        D = 256
        H = 16
        HD = D // H
        DFF = 4 * D
        LN_EPS = 1e-05

        def layernorm(x, gamma, beta):
            mu = jnp.mean(x, axis=-1, keepdims=True)
            var = jnp.mean(jnp.square(x - mu), axis=-1, keepdims=True)
            return (x - mu) * jax.lax.rsqrt(var + LN_EPS) * gamma + beta
        B, Nq, _ = q_x.shape
        Nk = kv_x.shape[1]
        scale = HD ** (-0.5)
        q = layernorm(q_x, ln_q_g, ln_q_b) @ Wq.T
        kv = layernorm(kv_x, ln_kv_g, ln_kv_b) @ Wkv.T
        q = q.reshape(B, Nq, H, HD).transpose(0, 2, 1, 3)
        kv = kv.reshape(B, Nk, 2, H, HD).transpose(2, 0, 3, 1, 4)
        k, v = (kv[0], kv[1])
        attn = jnp.einsum('bhqd,bhkd->bhqk', q, k) * scale
        attn = jax.nn.softmax(attn, axis=-1)
        out = jnp.einsum('bhqk,bhkd->bhqd', attn, v)
        out = out.transpose(0, 2, 1, 3).reshape(B, Nq, D)
        x = q_x + out @ Wo.T + bo
        h = jax.nn.silu(x @ W1.T + b1)
        x = x + h @ W2.T + b2
        return x
    x = _L0_xattn_ref(x, ctx_1024, L0_xattn_Wq, L0_xattn_Wkv, L0_xattn_Wo, L0_xattn_bo, L0_xattn_ln_q_g, L0_xattn_ln_q_b, L0_xattn_ln_kv_g, L0_xattn_ln_kv_b, L0_xattn_W1, L0_xattn_b1, L0_xattn_W2, L0_xattn_b2)
    return x

_drawn_inputs = setup_inputs


def setup_inputs(seed=0):
    import zlib

    import numpy as np

    out = dict(_drawn_inputs(seed))
    spreads = {'L0_xattn_bo': (0.0, 0.1),
     'L0_xattn_ln_q_g': (1.0, 0.6),
     'L0_xattn_ln_q_b': (0.0, 0.8),
     'L0_xattn_ln_kv_g': (1.0, 0.6),
     'L0_xattn_ln_kv_b': (0.0, 0.8),
     'L0_xattn_b1': (0.0, 0.271),
     'L0_xattn_b2': (0.0, 0.1)}
    factors = {'L0_xattn_Wq': 8.0}
    for name, (base, spread) in spreads.items():
        noise = np.random.default_rng([zlib.crc32(name.encode()), seed]).standard_normal(out[name].shape)
        drawn = base * np.exp(spread * noise) if base else spread * noise
        out[name] = jnp.asarray(drawn.astype(out[name].dtype))
    for name, factor in factors.items():
        out[name] = (out[name] * factor).astype(out[name].dtype)
    return out
```

```python
from contextlib import ExitStack

import concourse.bass as bass
from concourse import mybir

F32 = mybir.dt.float32
F32R = mybir.dt.float32r
ALU = mybir.AluOpType
ACT = mybir.ActivationFunctionType
AX = mybir.AxisListType

P = 128
B, NQ, NK, D = 4, 1024, 77, 256
H = 16
HD = D // H
DFF = 4 * D
C = 512
QT = C // P
KT = D // P
FT = DFF // P
NC = B * NQ // C
CPB = NQ // C
HPT = P // HD
NP = H // 2
QPT = P // 32
PTR = 4
KROWS = 96 + H
SCALE = HD ** -0.5
EPS = 1e-5
GQ, BQ, GKV, BKV, B1 = 0, KT, 2 * KT, 3 * KT, 4 * KT
NPAR = 4 * KT + FT


def step(c, d):
    i, u = c
    u += d
    return i + u // 2, u % 2


def first(c):
    return isinstance(c[0], int) and c == (0, 0)


def upto(c, n, k=0):
    i, u = c
    return i * (2 * n) + (n * u + k)


def build(nc, x, ctx_in, wqT, wkvT, woT, w1T, w2T, params, bo_d, b2_d, out):
    x_d = x.rearrange("b (h q p) d -> (b h) p q d", q=QT, p=P)
    out_d = out.rearrange("b (h q p) d -> (b h) p q d", q=QT, p=P)

    es = ExitStack()
    with es:
        def sb(name, shape, dt=F32):
            return es.enter_context(nc.sbuf_tensor(name, shape, dt))

        def sem(name):
            return es.enter_context(nc.semaphore(name))

        wq = [sb(f"wq_{s}", [P, KT, D], F32R) for s in ("hi", "lo")]
        wo = [sb(f"wo_{s}", [P, KT, D], F32R) for s in ("hi", "lo")]
        w1 = [sb(f"w1_{s}", [P, KT, DFF], F32R) for s in ("hi", "lo")]
        w2 = [sb(f"w2_{s}", [P, FT, D], F32R) for s in ("hi", "lo")]
        par = sb("par", [P, NPAR])
        q_bias = sb("q_bias", [P, KT])
        bo_row = sb("bo_row", [P, D])
        b2_row = sb("b2_row", [P, D])
        ident = sb("ident", [P, P])
        head_mask = sb("head_mask", [P, HPT])
        pick = sb("pick", [H, H, NK])
        neg_half = sb("neg_half", [P, QT])
        eps = sb("eps", [P, QT])
        k_split = [sb(f"k_{s}", [P, KT, B * NK], F32R) for s in ("hi", "lo")]
        k_diag = [sb(f"k_diag_{s}", [P, KT, HPT, NK], F32R) for s in ("hi", "lo")]
        k_stack = sb("k_stack", [KROWS, H, NK], F32R)
        v_all = sb("v_all", [NK, B, D])
        v_ones = sb("v_ones", [NK, H, 2, HD])
        xs = [sb(f"x_{u}", [P, QT, D]) for u in range(2)]
        stats = sb("stats", [P, QT, 6])
        mv = sb("mv", [P, QT, 2])
        var_eps = sb("var_eps", [P, QT])
        rstd = sb("rstd", [P, QT])
        xn = sb("xn", [P, QT, D])
        xt = [sb(f"xt_{s}", [P, KT, C], F32R) for s in ("hi", "lo")]
        qt = [sb(f"qt_{s}", [P, KT, C], F32R) for s in ("hi", "lo")]
        q_stack = sb("q_stack", [KROWS, NP, C], F32R)
        neg_max = sb("neg_max", [P, QT, H])
        neg_max_t = sb("neg_max_t", [H, C], F32R)
        probs = sb("probs", [P, PTR, 2, C])
        o_raw = sb("o_raw", [P, QT, C])
        rsum = sb("rsum", [P, QT, H])
        o_nat = xn
        x2 = [sb(f"x2_{u}", [P, QT, D]) for u in range(2)]
        x2t = [sb(f"x2t_{s}", [P, KT, C], F32R) for s in ("hi", "lo")]
        h_full = sb("h_full", [P, FT, C])
        h = [sb(f"h_{s}", [P, FT, C], F32R) for s in ("hi", "lo")]
        q_stack_v = q_stack[:, :, :].rearrange("p (t g) n -> p t g n", t=KT)
        k_stack_v = k_stack[:, :, :].rearrange("p (t g e) k -> p t g (e k)", t=KT, e=2)
        k_diag_v = [kd[:, :, :, :].rearrange("p t (g e) k -> p t g (e k)", e=2) for kd in k_diag]
        w1_raw = h_full[:, 0:4, :].rearrange("p f n -> p (f n)").rearrange("p (k n) -> p k n", k=KT)
        w2_raw = h_full[:, 4:8, :].rearrange("p f n -> p (f n)").rearrange("p (f n) -> p f n", f=FT)
        pv_flat = probs[:, :, :, :].rearrange("p a b n -> p (a b n)")
        wkv_raw = pv_flat[:, 0:1024].rearrange("p (k n) -> p k n", k=KT)
        wq_raw = pv_flat[:, 1024:1536].rearrange("p (k n) -> p k n", k=KT)
        wo_raw = pv_flat[:, 1536:2048].rearrange("p (k n) -> p k n", k=KT)
        or_flat = o_raw[:, :, :].rearrange("p a n -> p (a n)")
        ctx = or_flat[0:NK, 0:B * D].rearrange("p (b n) -> p b n", b=B)
        ctx_t = or_flat[:, B * D:B * D + KT * B * NK].rearrange("p (k n) -> p k n", k=KT)

        ps = es.enter_context(nc.psum_tensor("ps", [P, 8, 512], F32))
        PAIR = [ps[:, 0:2, :], ps[:, 2:4, :]]
        BANK = {"A": ps[:, 4, :], "B": ps[:, 5, :], "C": ps[:, 6, :], "D": ps[:, 7, :]}
        AB, CD = "AB", "CD"
        TURNED = [PAIR[0][:, 0, :], PAIR[1][:, 0, :]]
        PROJ = [PAIR[0][:, 1, :], PAIR[1][:, 1, :]]

        names = """ctx_loaded wkv_loaded wq_loaded wo_loaded w1_loaded w2_loaded par_loaded rows_loaded
            ident_zeroed ident_ready mask_set mask_low mask_ready pick_zeroed pick_ready pick_loaded half_set
            v_set ctx_stats ctx_mv ctx_var ctx_rstd ctx_normed ctx_ps ctx_t_ready
            kd_ps kd_hi_ready kd_lo_ready vd_ps v_ready qb_ps qb_ready wq_hi_ready wq_lo_ready
            wo_hi_ready wo_lo_ready w1_hi_ready w1_lo_ready w2_hi_ready w2_lo_ready
            k_diag_ready k_stack_loaded v_ones_ready
            stats_ready mv_ready var_ready rstd_ready xn_ready xbo_ready
            xt_ps xt_hi_ready xt_lo_ready q_ps q_hi_ready q_lo_ready q_stack_loaded
            s_ps max_ready mt_ps mt_ready st_ps exp_ready pv_ps o_raw_ready
            ot_ps rsum_ready o_nat_ready at_ps o_hi_ready o_lo_ready op_ps x2_ready
            x2t_ps x2_hi_ready x2_lo_ready x2b_ready h_ps h_full_ready h_hi_ready h_lo_ready
            y_ps y_ready""".split()
        S = {n: sem(n) for n in names}
        x_loaded = [sem(f"x_loaded_{u}") for u in range(2)]
        out_stored = [sem(f"out_stored_{u}") for u in range(2)]

        block = es.enter_context(nc.Block())
        FIRST = (0, 0)
        Q_DMAS, K_DMAS = 3 * QPT + 1, 3 * QPT
        SPLITS = ((0, 0), (0, 1), (1, 0))

        def f32(ap):
            return ap.bitcast(F32)

        def phases(eng, part1, part2):
            def phase(c, p=None):
                core = c if p is None or p < NC else None
                down = step(c, -2) if p is None or p >= 2 else None
                nxt = step(c, 1) if p is None or p + 1 < NC else None
                up = step(c, -1) if p is None or 1 <= p <= NC else None
                part1(core, down, nxt)
                part2(core, nxt, up, c[1] == 1)

            part2(None, FIRST, None, True)
            for p in (0, 1):
                phase((0, p), p)
            with eng.Fori(1, 3) as i:
                for u in range(2):
                    phase((i, u))
            for p in range(6, NC + 2):
                phase((p // 2, p % 2), p)

        @block.sync
        def _(sp):
            sp.dma_start(ctx, ctx_in.rearrange("b k d -> k b d")).then_inc(S["ctx_loaded"], 16)
            sp.dma_start(xs[0][:], x_d[0]).then_inc(x_loaded[0], 16)
            sp.dma_start(wq_raw, wqT).then_inc(S["wq_loaded"], 16)
            sp.dma_start(w1_raw, w1T).then_inc(S["w1_loaded"], 16)
            sp.dma_start(w2_raw, w2T).then_inc(S["w2_loaded"], 16)
            sp.dma_start(xs[1][:], x_d[1]).then_inc(x_loaded[1], 16)
            sp.wait_ge(S["pick_ready"], 1)
            sp.dma_start(f32(k_stack[96:KROWS, :, :]), pick[:]).then_inc(S["pick_loaded"], 16)

            def part1(core, down, nxt):
                if down is not None:
                    i, u = down
                    sp.wait_ge(S["y_ready"], upto(down, 2, 2))
                    sp.dma_start(out_d[i * 2 + u], x2[u][:]).then_inc(out_stored[u], 16)

            def part2(tail, front, up, new_batch):
                if front is None:
                    return
                if tail is not None:
                    sp.wait_ge(S["st_ps"], upto(tail, NP, NP))
                if new_batch:
                    sp.wait_ge(S["k_diag_ready"], front[0] * 4 + 4)
                    for r, s in enumerate((0, 0, 1)):
                        for g in range(QPT):
                            sp.dma_start(f32(k_stack_v[32 * r:32 * r + 32, :, g, :]),
                                         f32(k_diag_v[s][32 * g:32 * g + 32, :, g, :])
                                         ).then_inc(S["k_stack_loaded"], 16)
                for r, s, ready in ((0, 0, "q_hi_ready"), (2, 0, "q_hi_ready"), (1, 1, "q_lo_ready")):
                    sp.wait_ge(S[ready], upto(front, KT, KT))
                    for g in range(QPT):
                        sp.dma_start(f32(q_stack_v[32 * r:32 * r + 32, :, g, :]), f32(qt[s][32 * g:32 * g + 32, :, :])
                                     ).then_inc(S["q_stack_loaded"], 16)
                sp.wait_ge(S["mt_ready"], upto(front, 1, 1))
                sp.dma_start(f32(q_stack[96:KROWS, :, :]),
                             f32(neg_max_t[:]).unsqueeze(1).broadcast_to([H, NP, C])
                             ).then_inc(S["q_stack_loaded"], 16)
                i, u = step(front, 1)
                if tail is not None and not (isinstance(i, int) and i * 2 + u >= NC):
                    sp.wait_ge(S["x2_ready"], upto(tail, 2, 2))
                    sp.dma_start(xs[u][:], x_d[i * 2 + u]).then_inc(x_loaded[u], 16)

            phases(sp, part1, part2)
            for u in range(2):
                sp.wait_ge(out_stored[u], 16 * (NC // 2))

        @block.gpsimd
        def _(pool):
            pool.memset(ident[:], 0.0).then_inc(S["ident_zeroed"], 1)
            pool.memset(head_mask[:], 1.0).then_inc(S["mask_set"], 1)
            pool.memset(pick[:], 0.0).then_inc(S["pick_zeroed"], 1)
            pool.memset(neg_half[:], -0.5).then_inc(S["half_set"], 1)
            pool.memset(eps[:], EPS).then_inc(S["half_set"], 1)
            pool.memset(v_ones[:], 1.0).then_inc(S["v_set"], 1)
            pool.wait_ge(S["ident_zeroed"], 1)
            pool.affine_select(out=ident[:], in_=ident[:], compare_op=ALU.not_equal, fill=1.0, base=0,
                               pattern=[[-1, P]], channel_multiplier=1).then_inc(S["ident_ready"], 1)
            pool.wait_ge(S["mask_set"], 1)
            pool.affine_select(out=head_mask[:], in_=head_mask[:], compare_op=ALU.is_ge, fill=0.0, base=0,
                               pattern=[[-HD, HPT]], channel_multiplier=1).then_inc(S["mask_low"], 1)
            pool.wait_ge(S["mask_low"], 1)
            pool.affine_select(out=head_mask[:], in_=head_mask[:], compare_op=ALU.is_ge, fill=0.0,
                               base=HD - 1, pattern=[[HD, HPT]], channel_multiplier=-1
                               ).then_inc(S["mask_ready"], 1)
            pool.wait_ge(S["pick_zeroed"], 1)
            pool.affine_select(out=pick[:], in_=pick[:], compare_op=ALU.not_equal, fill=1.0, base=0,
                               pattern=[[-1, H], [0, NK]], channel_multiplier=1).then_inc(S["pick_ready"], 1)

            pool.wait_ge(S["half_set"], 2)
            pool.wait_ge(S["ctx_mv"], B)
            pool.tensor_scalar(var_eps[0:NK, :], mv[0:NK, :, 1], EPS, None, ALU.add).then_inc(S["ctx_var"], 1)
            pool.wait_ge(S["ctx_var"], 1)
            pool.tensor_tensor(rstd[0:NK, :], var_eps[0:NK, :], neg_half[0:NK, :], ALU.pow
                               ).then_inc(S["ctx_rstd"], 1)

            def norm(c):
                pool.wait_ge(S["mv_ready"], upto(c, QT, QT))
                pool.tensor_tensor(var_eps[:], mv[:, :, 1], eps[:], ALU.add).then_inc(S["var_ready"], 1)
                pool.wait_ge(S["var_ready"], upto(c, 1, 1))
                pool.tensor_tensor(rstd[:], var_eps[:], neg_half[:], ALU.pow).then_inc(S["rstd_ready"], 1)
                pool.wait_ge(S["xn_ready"], upto(c, QT, QT))
                _, u = c
                pool.tensor_tensor(xs[u][:], xs[u][:], bo_row[:].unsqueeze(1).broadcast_to([P, QT, D]),
                                   ALU.add).then_inc(S["xbo_ready"], 1)

            def lo(dst, raw, hi, ready, done):
                pool.wait_ge(S[ready], 1)
                pool.tensor_tensor(dst, raw, hi, ALU.subtract).then_inc(S[done], 1)

            pool.wait_ge(S["rows_loaded"], 32)
            norm(FIRST)
            lo(wo[1][:], wo_raw, f32(wo[0][:]), "wo_hi_ready", "wo_lo_ready")
            norm((0, 1))
            lo(w1[1][:], w1_raw, f32(w1[0][:]), "w1_hi_ready", "w1_lo_ready")
            lo(w2[1][:], w2_raw, f32(w2[0][:]), "w2_hi_ready", "w2_lo_ready")

            def part1(core, down, nxt):
                if nxt is not None and not (isinstance(nxt[0], int) and nxt[0] == 0):
                    norm(nxt)

            def part2(tail, front, up, new_batch):
                if tail is not None:
                    _, u = tail
                    pool.wait_ge(S["x2t_ps"], upto(tail, KT, KT))
                    pool.tensor_tensor(x2[u][:], x2[u][:], b2_row[:].unsqueeze(1).broadcast_to([P, QT, D]),
                                       ALU.add).then_inc(S["x2b_ready"], 1)

            phases(pool, part1, part2)

        @block.scalar
        def _(act):
            act.dma_start(wkv_raw, wkvT).then_inc(S["wkv_loaded"], 16)
            act.dma_start(par[:], params).then_inc(S["par_loaded"], 16)
            act.dma_start(wo_raw, woT).then_inc(S["wo_loaded"], 16)
            act.dma_start(bo_row[:], bo_d).then_inc(S["rows_loaded"], 16)
            act.dma_start(b2_row[:], b2_d).then_inc(S["rows_loaded"], 16)

            for b in range(B):
                act.wait_ge(S["vd_ps"], b + 1)
                act.activation(v_all[:, b, :], BANK["AB"[b % 2]][0:NK, 0:D], ACT.Copy).then_inc(S["v_ready"], 1)

            def weights_hi():
                for w, raw, name in ((wo, wo_raw, "wo"), (w1, w1_raw, "w1"), (w2, w2_raw, "w2")):
                    act.wait_ge(S[name + "_loaded"], 16)
                    act.activation(w[0][:], raw, ACT.Copy).then_inc(S[name + "_hi_ready"], 1)

            def part1(core, down, nxt):
                if core is None:
                    return
                if first(core):
                    act.wait_ge(S["wq_lo_ready"], KT)
                    act.wait_ge(S["wo_lo_ready"], 1)
                for g in range(NP):
                    act.wait_ge(S["st_ps"], upto(core, NP, g + 1))
                    if g >= PTR:
                        act.wait_ge(S["pv_ps"], upto(core, QT, (g - PTR) // 2 + 1))
                    act.activation(probs[0:NK, g % PTR, :, :], PAIR[g % 2][0:NK], ACT.Exp, scale=SCALE
                                   ).then_inc(S["exp_ready"], 1)

            def part2(tail, front, up, new_batch):
                def silu(*fs):
                    if up is None:
                        return
                    for f in fs:
                        if f == 0:
                            if first(up):
                                act.wait_ge(S["w1_lo_ready"], 1)
                                act.wait_ge(S["w2_lo_ready"], 1)
                            else:
                                act.wait_ge(S["h_lo_ready"], upto(step(up, -1), FT // 2, FT // 2))
                        act.wait_ge(S["h_ps"], upto(up, FT, f + 1))
                        act.activation(h_full[:, f, :], BANK[CD[f % 2]], ACT.Silu,
                                       bias=par[:, B1 + f:B1 + f + 1]).then_inc(S["h_full_ready"], 1)

                if front is not None:
                    if new_batch:
                        b = front[0]
                        if tail is None:
                            act.wait_ge(S["v_set"], 1)
                            act.wait_ge(S["v_ready"], B)
                        else:
                            act.wait_ge(S["pv_ps"], upto(tail, QT, QT))
                        act.activation(v_ones[:, :, 0, :],
                                       v_all[:, bass.ds(b, 1), :].rearrange("k o (h d) -> k (o h) d", d=HD), ACT.Copy
                                       ).then_inc(S["v_ones_ready"], 1)
                    for k in range(KT):
                        act.wait_ge(S["xt_ps"], upto(front, KT, k + 1))
                        act.activation(xt[0][:, k, :], TURNED[k], ACT.Copy).then_inc(S["xt_hi_ready"], 1)
                silu(0, 1)
                if front is not None:
                    if tail is None:
                        act.wait_ge(S["qb_ready"], 1)
                    for t in range(KT):
                        act.wait_ge(S["q_ps"], upto(front, KT, t + 1))
                        act.activation(qt[0][:, t, :], PROJ[t], ACT.Identity, bias=q_bias[:, t:t + 1]
                                       ).then_inc(S["q_hi_ready"], 1)
                if tail is None and front is not None:
                    weights_hi()
                silu(2)
                if tail is not None:
                    for k in range(KT):
                        act.wait_ge(S["at_ps"], upto(tail, KT, k + 1))
                        act.activation(xt[0][:, k, :], BANK[AB[k]], ACT.Copy).then_inc(S["o_hi_ready"], 1)
                silu(3, 4, 5, 6, 7)
                if tail is not None:
                    for k in range(KT):
                        act.wait_ge(S["x2t_ps"], upto(tail, KT, k + 1))
                        act.activation(x2t[0][:, k, :], BANK[AB[k]], ACT.Copy).then_inc(S["x2_hi_ready"], 1)

            phases(act, part1, part2)

        @block.vector
        def _(dve):
            dve.wait_ge(S["ctx_loaded"], 16)
            for b in range(B):
                dve.bn_stats(stats[0:NK, b, :], ctx[:, b, :]).then_inc(S["ctx_stats"], 1)
            for b in range(B):
                dve.wait_ge(S["ctx_stats"], b + 1)
                dve.bn_aggr(mv[0:NK, b, :], stats[0:NK, b, :]).then_inc(S["ctx_mv"], 1)
            dve.wait_ge(S["ctx_rstd"], 1)
            for b in range(B):
                dve.tensor_scalar(ctx[:, b, :], ctx[:, b, :], mv[0:NK, b, 0:1], rstd[0:NK, b:b + 1],
                                  ALU.subtract, ALU.mult).then_inc(S["ctx_normed"], 1)

            def stats_of(c):
                i, u = c
                dve.wait_ge(x_loaded[u], i * 16 + 16)
                for q in range(QT):
                    dve.bn_stats(stats[:, q, :], xs[u][:, q, :]).then_inc(S["stats_ready"], 1)
                dve.wait_ge(S["stats_ready"], upto(c, QT, QT))

            def mean_var(c):
                for q in range(QT):
                    dve.bn_aggr(mv[:, q, :], stats[:, q, :]).then_inc(S["mv_ready"], 1)

            def normalise(c):
                _, u = c
                dve.wait_ge(S["rstd_ready"], upto(c, 1, 1))
                for q in range(QT):
                    dve.tensor_scalar(xn[:, q, :], xs[u][:, q, :], mv[:, q, 0:1], rstd[:, q:q + 1],
                                      ALU.subtract, ALU.mult).then_inc(S["xn_ready"], 1)

            stats_of(FIRST)
            mean_var(FIRST)
            dve.wait_ge(S["par_loaded"], 16)
            for k in range(KT):
                dve.wait_ge(S["ctx_ps"], k + 1)
                dve.tensor_scalar(ctx_t[:, k, :], BANK[AB[k]][:, 0:B * NK], par[:, GKV + k:GKV + k + 1],
                                  par[:, BKV + k:BKV + k + 1], ALU.mult, ALU.add).then_inc(S["ctx_t_ready"], 1)
            normalise(FIRST)
            for t in range(KT):
                dve.wait_ge(S["kd_ps"], t + 1)
                dve.tensor_copy(k_split[0][:, t, :], BANK[CD[t]][:, 0:B * NK]).then_inc(S["kd_hi_ready"], 1)
            for t in range(KT):
                dve.wait_ge(S["kd_hi_ready"], t + 1)
                dve.tensor_tensor(k_split[1][:, t, :], BANK[CD[t]][:, 0:B * NK], f32(k_split[0][:, t, :]),
                                  ALU.subtract).then_inc(S["kd_lo_ready"], 1)
            dve.wait_ge(S["wq_loaded"], 16)
            for k in range(KT):
                dve.tensor_scalar(wq[0][:, k, :], wq_raw[:, k, :], par[:, GQ + k:GQ + k + 1], None, ALU.mult
                                  ).then_inc(S["wq_hi_ready"], 1)
            for k in range(KT):
                dve.wait_ge(S["wq_hi_ready"], k + 1)
                dve.scalar_tensor_tensor(out=wq[1][:, k, :], in0=wq_raw[:, k, :], scalar=par[:, GQ + k:GQ + k + 1],
                                         in1=f32(wq[0][:, k, :]), op0=ALU.mult, op1=ALU.subtract
                                         ).then_inc(S["wq_lo_ready"], 1)
            dve.wait_ge(S["qb_ps"], 1)
            dve.tensor_copy(q_bias[:], BANK["C"][:, 0:KT]).then_inc(S["qb_ready"], 1)
            dve.wait_ge(S["mask_ready"], 1)
            dve.wait_ge(S["kd_lo_ready"], KT)

            def split_h(c, g):
                if g == 0 and not first(c):
                    dve.wait_ge(S["y_ps"], upto(step(c, -1), 2, 2))
                t = slice(2 * g, 2 * g + 2)
                dve.wait_ge(S["h_full_ready"], upto(c, FT, 2 * g + 2))
                dve.tensor_copy(h[0][:, t, :], h_full[:, t, :]).then_inc(S["h_hi_ready"], 1)
                dve.wait_ge(S["h_hi_ready"], upto(c, FT // 2, g + 1))
                dve.tensor_tensor(h[1][:, t, :], h_full[:, t, :], f32(h[0][:, t, :]), ALU.subtract
                                  ).then_inc(S["h_lo_ready"], 1)

            def save_o(c, *js):
                if c is not None:
                    for j in js:
                        dve.wait_ge(S["pv_ps"], upto(c, QT, j + 1))
                        dve.tensor_copy(o_raw[:, j, :], BANK[AB[j % 2]]).then_inc(S["o_raw_ready"], 1)

            def part1(core, down, nxt):
                if nxt is not None:
                    stats_of(nxt)
                if down is not None:
                    split_h(down, 3)
                if nxt is not None:
                    mean_var(nxt)
                save_o(core, 0)
                if nxt is not None:
                    normalise(nxt)
                save_o(core, 1)
                if down is not None:
                    _, u = down
                    dve.wait_ge(S["x2b_ready"], upto(down, 1, 1))
                    for s in range(2):
                        dve.wait_ge(S["y_ps"], upto(down, 2, s + 1))
                        y = x2[u][:, 2 * s:2 * s + 2, :]
                        dve.tensor_tensor(y, BANK[CD[s]].rearrange("p (q d) -> p q d", q=2), y, ALU.add
                                          ).then_inc(S["y_ready"], 1)

            def part2(tail, front, up, new_batch):
                def find_max(q):
                    for t in range(KT):
                        dve.wait_ge(S["s_ps"], upto(front, QT * KT, KT * q + t + 1))
                        dve.tensor_reduce(neg_max[:, q, HPT * t:HPT * t + HPT].rearrange("p (a h) -> p a h", a=2),
                                          PAIR[t][:, :, 0:HPT // 2 * NK].rearrange("p a (h k) -> p a h k", k=NK),
                                          AX.X, ALU.max, negate=True).then_inc(S["max_ready"], 1)

                if front is not None:
                    if new_batch:
                        b = front[0]
                        for s in range(2):
                            for t in range(KT):
                                kd = f32(k_split[s][:, t, bass.ds(b * NK, NK)])
                                dve.tensor_tensor(k_diag[s][:, t, :, :], kd.unsqueeze(1).broadcast_to([P, HPT, NK]),
                                                  head_mask[:].unsqueeze(2).broadcast_to([P, HPT, NK]), ALU.mult
                                                  ).then_inc(S["k_diag_ready"], 1)
                for k in range(KT):
                    save_o(tail, 2 + k)
                    if front is not None:
                        dve.wait_ge(S["xt_hi_ready"], upto(front, KT, k + 1))
                        dve.tensor_tensor(xt[1][:, k, :], TURNED[k], f32(xt[0][:, k, :]), ALU.subtract
                                          ).then_inc(S["xt_lo_ready"], 1)
                if tail is not None:
                    for q in range(QT):
                        dve.wait_ge(S["ot_ps"], upto(tail, QT, q + 1))
                        o_v = BANK[AB[q % 2]].rearrange("p (h e d) -> p h e d", h=H, e=2)
                        dve.reciprocal(rsum[:, q, :], o_v[:, :, 1, 0]).then_inc(S["rsum_ready"], 1)
                        dve.wait_ge(S["rsum_ready"], upto(tail, QT, q + 1))
                        dve.tensor_tensor(o_nat[:, q, :].rearrange("p (h d) -> p h d", h=H), o_v[:, :, 0, :],
                                          rsum[:, q, :].unsqueeze(2).broadcast_to([P, H, HD]), ALU.mult
                                          ).then_inc(S["o_nat_ready"], 1)
                if up is not None:
                    split_h(up, 0)
                if front is not None:
                    for t in range(KT):
                        dve.wait_ge(S["q_hi_ready"], upto(front, KT, t + 1))
                        dve.scalar_tensor_tensor(out=qt[1][:, t, :], in0=PROJ[t], scalar=q_bias[:, t:t + 1],
                                                 in1=f32(qt[0][:, t, :]), op0=ALU.add, op1=ALU.subtract
                                                 ).then_inc(S["q_lo_ready"], 1)
                if tail is not None:
                    for k in range(KT):
                        dve.wait_ge(S["o_hi_ready"], upto(tail, KT, k + 1))
                        dve.tensor_tensor(xt[1][:, k, :], BANK[AB[k]], f32(xt[0][:, k, :]), ALU.subtract
                                          ).then_inc(S["o_lo_ready"], 1)
                if front is not None:
                    find_max(0)
                if tail is not None:
                    i, u = tail
                    if not (isinstance(i, int) and i == 0):
                        dve.wait_ge(out_stored[u], i * 16)
                    dve.wait_ge(S["xbo_ready"], upto(tail, 1, 1))
                    for s in range(2):
                        dve.wait_ge(S["op_ps"], upto(tail, 2, s + 1))
                        q = slice(2 * s, 2 * s + 2)
                        dve.tensor_tensor(x2[u][:, q, :], BANK[AB[s]].rearrange("p (q d) -> p q d", q=2),
                                          xs[u][:, q, :], ALU.add).then_inc(S["x2_ready"], 1)
                if up is not None:
                    split_h(up, 1)
                if front is not None:
                    find_max(1)
                    find_max(2)
                if up is not None:
                    split_h(up, 2)
                if front is not None:
                    find_max(3)
                    dve.wait_ge(S["mt_ps"], upto(front, 1, 1))
                    dve.tensor_copy(neg_max_t[:], TURNED[0][0:H, :]).then_inc(S["mt_ready"], 1)
                if tail is not None:
                    for k in range(KT):
                        dve.wait_ge(S["x2_hi_ready"], upto(tail, KT, k + 1))
                        dve.tensor_tensor(x2t[1][:, k, :], BANK[AB[k]], f32(x2t[0][:, k, :]), ALU.subtract
                                          ).then_inc(S["x2_lo_ready"], 1)

            phases(dve, part1, part2)

        @block.tensor
        def _(pe):
            def turn(dst, src, n=P):
                return pe.transpose(dst, src, ident[0:n, 0:n])

            pe.wait_ge(S["ident_ready"], 1)
            for k in range(KT):
                for b in range(B):
                    pe.wait_ge(S["ctx_normed"], b + 1)
                    last = turn(BANK[AB[k]][:, b * NK:(b + 1) * NK], ctx[:, b, k * P:(k + 1) * P], NK)
                last.then_inc(S["ctx_ps"], 1)
            pe.wait_ge(S["ctx_t_ready"], KT)
            pe.wait_ge(S["wkv_loaded"], 16)
            for t in range(KT):
                for k in range(KT):
                    last = pe.matmul(BANK[CD[t]][:, 0:B * NK], wkv_raw[:, k, t * P:(t + 1) * P], ctx_t[:, k, :],
                                     start=(k == 0), stop=(k == KT - 1))
                last.then_inc(S["kd_ps"], 1)
            for b in range(B):
                if b >= 2:
                    pe.wait_ge(S["v_ready"], b - 1)
                for k in range(KT):
                    last = pe.matmul(BANK[AB[b % 2]][0:NK, 0:D], ctx_t[:, k, b * NK:(b + 1) * NK],
                                     wkv_raw[:, k, D:2 * D], start=(k == 0), stop=(k == KT - 1))
                last.then_inc(S["vd_ps"], 1)
            pe.wait_ge(S["wq_loaded"], 16)
            pe.wait_ge(S["kd_lo_ready"], KT)
            for t in range(KT):
                for k in range(KT):
                    last = pe.matmul(BANK["C"][:, t:t + 1], wq_raw[:, k, t * P:(t + 1) * P],
                                     par[:, BQ + k:BQ + k + 1], start=(k == 0), stop=(k == KT - 1))
            last.then_inc(S["qb_ps"], 1)

            def values(core, j):
                if j == 0 and core[1] == 0:
                    pe.wait_ge(S["v_ones_ready"], core[0] + 1)
                if j == 0 and not first(core):
                    pe.wait_ge(S["x2_lo_ready"], upto(step(core, -1), KT, KT))
                if j >= 2:
                    pe.wait_ge(S["o_raw_ready"], upto(core, QT, j - 1))
                pe.wait_ge(S["exp_ready"], upto(core, NP, 2 * j + 2))
                for n in range(4):
                    last = pe.matmul(BANK[AB[j % 2]][32 * n:32 * n + 32, :],
                                     v_ones[:, 4 * j + n, :, :].rearrange("k e d -> k (e d)"),
                                     probs[0:NK, (2 * j + n // 2) % PTR, n % 2, :], start=True, stop=True,
                                     tile_position=(0, 32 * n))
                last.then_inc(S["pv_ps"], 1)

            def part1(core, down, nxt):
                def down_tile(f):
                    if down is None:
                        return
                    if f == 0:
                        pe.wait_ge(S["h_full_ready"], upto(down, FT, FT))
                        if first(down):
                            pe.wait_ge(S["w2_lo_ready"], 1)
                    if f % 2 == 0:
                        pe.wait_ge(S["h_lo_ready"], upto(down, FT // 2, f // 2 + 1))
                    for s in range(2):
                        for q in range(2):
                            for n, (a, w) in enumerate(SPLITS):
                                last = pe.matmul(BANK[CD[s]][:, q * D:(q + 1) * D],
                                                 h[a][:, f, (2 * s + q) * P:(2 * s + q + 1) * P], w2[w][:, f, :],
                                                 start=(f == 0 and q == 0 and n == 0), stop=(f == FT - 1 and n == 2),
                                                 skip_group_check=True)
                        if f == FT - 1:
                            last.then_inc(S["y_ps"], 1)

                down_tile(0)
                for g in range(NP):
                    if core is not None:
                        if g == 0:
                            pe.wait_ge(S["q_stack_loaded"], upto(core, Q_DMAS * 16, Q_DMAS * 16))
                            if first(core):
                                pe.wait_ge(S["pick_loaded"], 16)
                            if core[1] == 0:
                                pe.wait_ge(S["k_stack_loaded"], core[0] * (K_DMAS * 16) + K_DMAS * 16)
                        if g >= 2:
                            pe.wait_ge(S["exp_ready"], upto(core, NP, g - 1))
                        for e in range(2):
                            last = pe.matmul(PAIR[g % 2][0:NK, e, :], k_stack[:, 2 * g + e, :], q_stack[:, g, :],
                                             start=True, stop=True)
                        last.then_inc(S["st_ps"], 1)
                    if g + 1 < FT:
                        down_tile(g + 1)
                    if core is not None and g % 2 == 1 and g >= 3:
                        values(core, (g - 3) // 2)

            def part2(tail, front, up, new_batch):
                def up_tiles(*fs):
                    if up is None:
                        return
                    for f in fs:
                        if f == 0:
                            pe.wait_ge(S["x2_lo_ready"], upto(up, KT, KT))
                            if first(up):
                                pe.wait_ge(S["w1_lo_ready"], 1)
                        if f < 2:
                            if not first(up):
                                pe.wait_ge(S["y_ready"], upto(step(up, -1), 2, f + 1))
                        else:
                            pe.wait_ge(S["h_full_ready"], upto(up, FT, f - 1))
                        for n, (w, a) in enumerate(SPLITS):
                            for k in range(KT):
                                last = pe.matmul(BANK[CD[f % 2]], w1[w][:, k, f * P:(f + 1) * P], x2t[a][:, k, :],
                                                 start=(n == 0 and k == 0), stop=(n == 2 and k == KT - 1))
                        last.then_inc(S["h_ps"], 1)

                def turn_o(*qs):
                    if tail is None:
                        return
                    for q in qs:
                        if q == 0:
                            pe.wait_ge(S["o_raw_ready"], upto(tail, QT, QT))
                        if q >= 2:
                            pe.wait_ge(S["o_nat_ready"], upto(tail, QT, q - 1))
                        for j in range(QT):
                            last = turn(BANK[AB[q % 2]][:, j * P:(j + 1) * P], o_raw[:, j, q * P:(q + 1) * P])
                        last.then_inc(S["ot_ps"], 1)

                def scores(q):
                    if front is None:
                        return
                    for t in range(KT):
                        if q > 0:
                            pe.wait_ge(S["max_ready"], upto(front, QT * KT, KT * (q - 1) + t + 1))
                        else:
                            pe.wait_ge(S["q_lo_ready"], upto(front, KT, t + 1))
                            if new_batch:
                                pe.wait_ge(S["k_diag_ready"], front[0] * 4 + t + 1)
                        for a in range(2):
                            last = pe.matmul(PAIR[t][:, a, 0:HPT // 2 * NK], qt[0][:, t, q * P:(q + 1) * P],
                                             k_diag[0][:, t, HPT // 2 * a:HPT // 2 * (a + 1), :],
                                             start=True, stop=True)
                        last.then_inc(S["s_ps"], 1)

                def turn_x(k):
                    if front is None:
                        return
                    if tail is not None:
                        pe.wait_ge(S["exp_ready"], upto(tail, NP, NP - 1 + k))
                    pe.wait_ge(S["xn_ready"], upto(front, QT, QT))
                    for q in range(QT):
                        last = turn(TURNED[k][:, q * P:(q + 1) * P], xn[:, q, k * P:(k + 1) * P])
                    last.then_inc(S["xt_ps"], 1)

                turn_x(0)
                if tail is not None:
                    values(tail, 3)
                turn_x(1)
                up_tiles(0)
                turn_o(0, 1)
                up_tiles(1)
                turn_o(2, 3)
                if front is not None:
                    if tail is None:
                        pe.wait_ge(S["wq_lo_ready"], KT)
                    pe.wait_ge(S["xt_lo_ready"], upto(front, KT, KT))
                    for t in range(KT):
                        for n, (w, a) in enumerate(SPLITS):
                            for k in range(KT):
                                last = pe.matmul(PROJ[t], wq[w][:, k, t * P:(t + 1) * P], xt[a][:, k, :],
                                                 start=(n == 0 and k == 0), stop=(n == 2 and k == KT - 1))
                        last.then_inc(S["q_ps"], 1)
                up_tiles(2)
                if tail is not None:
                    pe.wait_ge(S["o_nat_ready"], upto(tail, QT, QT))
                    for k in range(KT):
                        for q in range(QT):
                            last = turn(BANK[AB[k]][:, q * P:(q + 1) * P], o_nat[:, q, k * P:(k + 1) * P])
                        last.then_inc(S["at_ps"], 1)
                up_tiles(3)
                scores(0)
                if tail is not None:
                    if first(tail):
                        pe.wait_ge(S["wo_lo_ready"], 1)
                    pe.wait_ge(S["o_lo_ready"], upto(tail, KT, KT))
                    for s in range(2):
                        for q in range(2):
                            m = 0
                            for a, w in SPLITS:
                                for k in range(KT):
                                    last = pe.matmul(BANK[AB[s]][:, q * D:(q + 1) * D],
                                                     xt[a][:, k, (2 * s + q) * P:(2 * s + q + 1) * P], wo[w][:, k, :],
                                                     start=(m == 0), stop=(m == 3 * KT - 1))
                                    m += 1
                        last.then_inc(S["op_ps"], 1)
                up_tiles(4)
                scores(1)
                up_tiles(5)
                scores(2)
                up_tiles(6)
                scores(3)
                up_tiles(7)
                if front is not None:
                    pe.wait_ge(S["max_ready"], upto(front, QT * KT, QT * KT))
                    for q in range(QT):
                        last = turn(TURNED[0][0:H, q * P:(q + 1) * P], neg_max[:, q, :])
                    last.then_inc(S["mt_ps"], 1)
                if tail is not None:
                    pe.wait_ge(S["x2_ready"], upto(tail, 2, 2))
                    _, u = tail
                    for k in range(KT):
                        for q in range(QT):
                            last = turn(BANK[AB[k]][:, q * P:(q + 1) * P], x2[u][:, q, k * P:(k + 1) * P])
                        last.then_inc(S["x2t_ps"], 1)

            phases(pe, part1, part2)


def kernel(**inputs):
    import numpy as np
    import concourse.bacc as bacc
    from concourse.bass_utils import run_bass_kernel_spmd as run

    a = {k.replace("L0_xattn_", ""): np.asarray(v) for k, v in inputs.items()}

    def by_rows(w):
        return np.ascontiguousarray(w.T.reshape(-1, P, w.shape[0]).transpose(1, 0, 2))

    def columns(v):
        return v.reshape(-1, P).T

    arrays = {
        "x": a["x"], "ctx": a["ctx_1024"],
        "wqT": by_rows(a["Wq"]), "wkvT": by_rows(a["Wkv"]), "woT": by_rows(a["Wo"]),
        "w1T": by_rows(a["W1"]), "w2T": by_rows(a["W2"]),
        "params": np.concatenate([columns(a[n]) for n in ("ln_q_g", "ln_q_b", "ln_kv_g", "ln_kv_b", "b1")], axis=1),
        "bo": np.broadcast_to(a["bo"], (P, D)), "b2": np.broadcast_to(a["b2"], (P, D)),
    }
    arrays = {f"in_{k}": np.ascontiguousarray(v) for k, v in arrays.items()}
    nc = bacc.Bacc("TRN2", target_bir_lowering=False, num_devices=1)
    args = [nc.dram_tensor(k, v.shape, mybir.dt.from_np(v.dtype), kind="ExternalInput").ap()
            for k, v in arrays.items()]
    out = nc.dram_tensor("out", (B, NQ, D), F32, kind="ExternalOutput").ap()
    build(nc, *args, out)
    r = run(nc, [arrays], core_ids=[0])
    return r.results[0]["out"]
```

```python
from contextlib import ExitStack

import concourse.bass as bass
from concourse import mybir

F32 = mybir.dt.float32
F32R = mybir.dt.float32r
ALU = mybir.AluOpType
ACT = mybir.ActivationFunctionType
AX = mybir.AxisListType

P = 128
B, NQ, NK, D = 4, 1024, 77, 256
H = 16
HD = D // H
DFF = 4 * D
C = 512
QT = C // P
KT = D // P
FT = DFF // P
NC = B * NQ // C
CPB = NQ // C
HPT = P // HD
NP = H // 2
QPT = P // 32
PTR = 4
KROWS = 96 + H
SCALE = HD ** -0.5
EPS = 1e-5
GQ, BQ, GKV, BKV, B1 = 0, KT, 2 * KT, 3 * KT, 4 * KT
NPAR = 4 * KT + FT


def step(c, d):
    i, u = c
    u += d
    return i + u // 2, u % 2


def first(c):
    return isinstance(c[0], int) and c == (0, 0)


def upto(c, n, k=0):
    i, u = c
    return i * (2 * n) + (n * u + k)


def build(nc, x, ctx_in, wqT, wkvT, woT, w1T, w2T, params, bo_d, b2_d, out):
    x_d = x.rearrange("b (h q p) d -> (b h) p q d", q=QT, p=P)
    out_d = out.rearrange("b (h q p) d -> (b h) p q d", q=QT, p=P)

    es = ExitStack()
    with es:
        def sb(name, shape, dt=F32):
            return es.enter_context(nc.sbuf_tensor(name, shape, dt))

        def sem(name):
            return es.enter_context(nc.semaphore(name))

        wq = [sb(f"wq_{s}", [P, KT, D], F32R) for s in ("hi", "lo")]
        wo = [sb(f"wo_{s}", [P, KT, D], F32R) for s in ("hi", "lo")]
        w1 = [sb(f"w1_{s}", [P, KT, DFF], F32R) for s in ("hi", "lo")]
        w2 = [sb(f"w2_{s}", [P, FT, D], F32R) for s in ("hi", "lo")]
        par = sb("par", [P, NPAR])
        q_bias = sb("q_bias", [P, KT])
        bo_row = sb("bo_row", [P, D])
        b2_row = sb("b2_row", [P, D])
        ident = sb("ident", [P, P])
        head_mask = sb("head_mask", [P, HPT])
        pick = sb("pick", [H, H, NK])
        neg_half = sb("neg_half", [P, QT])
        eps = sb("eps", [P, QT])
        k_split = [sb(f"k_{s}", [P, KT, B * NK], F32R) for s in ("hi", "lo")]
        k_diag = [sb(f"k_diag_{s}", [P, KT, HPT, NK], F32R) for s in ("hi", "lo")]
        k_stack = sb("k_stack", [KROWS, H, NK], F32R)
        v_all = sb("v_all", [NK, B, D])
        v_ones = sb("v_ones", [NK, H, 2, HD])
        xs = [sb(f"x_{u}", [P, QT, D]) for u in range(2)]
        stats = sb("stats", [P, QT, 6])
        mv = sb("mv", [P, QT, 2])
        var_eps = sb("var_eps", [P, QT])
        rstd = sb("rstd", [P, QT])
        ctx_mv = sb("ctx_mv", [NK, B, 2])
        ctx_rstd = sb("ctx_rstd", [NK, B])
        xn = sb("xn", [P, QT, D])
        xt = [sb(f"xt_{s}", [P, KT, C], F32R) for s in ("hi", "lo")]
        qt = [sb(f"qt_{s}", [P, KT, C], F32R) for s in ("hi", "lo")]
        q_stack = sb("q_stack", [KROWS, NP, C], F32R)
        neg_max = sb("neg_max", [P, QT, H])
        neg_max_t = sb("neg_max_t", [H, C], F32R)
        probs = sb("probs", [P, PTR, 2, C])
        o_raw = sb("o_raw", [P, QT, C])
        rsum = sb("rsum", [P, QT, H])
        o_nat = xn
        x2 = [sb(f"x2_{u}", [P, QT, D]) for u in range(2)]
        x2t = [sb(f"x2t_{s}", [P, KT, C], F32R) for s in ("hi", "lo")]
        h_full = sb("h_full", [P, FT, C])
        h = [sb(f"h_{s}", [P, FT, C], F32R) for s in ("hi", "lo")]
        q_stack_v = q_stack[:, :, :].rearrange("p (t g) n -> p t g n", t=KT)
        k_stack_v = k_stack[:, :, :].rearrange("p (t g e) k -> p t g (e k)", t=KT, e=2)
        k_diag_v = [kd[:, :, :, :].rearrange("p t (g e) k -> p t g (e k)", e=2) for kd in k_diag]
        w1_raw = h_full[:, 0:4, :].rearrange("p f n -> p (f n)").rearrange("p (k n) -> p k n", k=KT)
        w2_raw = h_full[:, 4:8, :].rearrange("p f n -> p (f n)").rearrange("p (f n) -> p f n", f=FT)
        pv_flat = probs[:, :, :, :].rearrange("p a b n -> p (a b n)")
        wkv_raw = pv_flat[:, 0:1024].rearrange("p (k n) -> p k n", k=KT)
        wq_raw = pv_flat[:, 1024:1536].rearrange("p (k n) -> p k n", k=KT)
        wo_raw = pv_flat[:, 1536:2048].rearrange("p (k n) -> p k n", k=KT)
        or_flat = o_raw[:, :, :].rearrange("p a n -> p (a n)")
        ctx = or_flat[0:NK, 0:B * D].rearrange("p (b n) -> p b n", b=B)
        ctx_t = or_flat[:, B * D:B * D + KT * B * NK].rearrange("p (k n) -> p k n", k=KT)

        ps = es.enter_context(nc.psum_tensor("ps", [P, 8, 512], F32))
        PAIR = [ps[:, 0:2, :], ps[:, 2:4, :]]
        BANK = {"A": ps[:, 4, :], "B": ps[:, 5, :], "C": ps[:, 6, :], "D": ps[:, 7, :]}
        AB, CD = "AB", "CD"
        CD_BANKS = [BANK["C"], BANK["D"]]
        TURNED = [PAIR[0][:, 0, :], PAIR[1][:, 0, :]]
        PROJ = [PAIR[0][:, 1, :], PAIR[1][:, 1, :]]

        names = """ctx_loaded wkv_loaded wq_loaded wo_loaded w1_loaded w2_loaded par_loaded rows_loaded
            ident_zeroed ident_ready mask_set mask_low mask_ready pick_zeroed pick_ready pick_loaded half_set
            v_set ctx_stats ctx_mv ctx_var ctx_rstd ctx_normed ctx_ps ctx_t_ready
            kd_ps kd_hi_ready kd_lo_ready vd_ps v_ready qb_ps qb_ready wq_hi_ready wq_lo_ready
            wo_hi_ready wo_lo_ready w1_hi_ready w1_lo_ready w2_hi_ready w2_lo_ready
            first_diag_ready first_k_loaded first_third_loaded k_diag_ready k_stack_loaded v_ones_ready
            stats_ready mv_ready var_ready rstd_ready xn_ready xbo_ready
            xt_ps xt_hi_ready xt_lo_ready q_ps q_hi_ready q_lo_ready q_stack_loaded
            s_ps max_ready mt_ps mt_ready st_ps exp_ready pv_ps o_raw_ready
            ot_ps rsum_ready o_nat_ready at_ps o_hi_ready o_lo_ready op_ps x2_ready
            x2t_ps x2_hi_ready x2_lo_ready x2b_ready h_ps h_full_ready h_hi_ready h_lo_ready
            y_ps y_ready""".split()
        S = {n: sem(n) for n in names}
        x_loaded = [sem(f"x_loaded_{u}") for u in range(2)]
        out_stored = [sem(f"out_stored_{u}") for u in range(2)]

        block = es.enter_context(nc.Block())
        FIRST = (0, 0)
        Q_DMAS, K_DMAS = 3 * QPT + 1, 3 * QPT
        SPLITS = ((0, 0), (0, 1), (1, 0))

        def f32(ap):
            return ap.bitcast(F32)

        def stack_keys(eng, r, loaded):
            for g in range(QPT):
                eng.dma_start(f32(k_stack_v[32 * r:32 * r + 32, :, g, :]),
                              f32(k_diag_v[r // 2][32 * g:32 * g + 32, :, g, :])
                              ).then_inc(S[loaded], 16)

        def early(front):
            return front is not None and isinstance(front[0], int) and front in ((0, 1), (1, 0))

        def phases(eng, part1, part2):
            def phase(c, p=None):
                core = c if p is None or p < NC else None
                down = step(c, -2) if p is None or p >= 2 else None
                nxt = step(c, 1) if p is None or p + 1 < NC else None
                up = step(c, -1) if p is None or 1 <= p <= NC else None
                part1(core, down, nxt)
                part2(core, nxt, up, c[1] == 1)

            for p in (0, 1):
                phase((0, p), p)
            with eng.Fori(1, 3) as i:
                for u in range(2):
                    phase((i, u))
            for p in range(6, NC + 2):
                phase((p // 2, p % 2), p)

        @block.sync
        def _(sp):
            sp.dma_start(ctx, ctx_in.rearrange("b k d -> k b d")).then_inc(S["ctx_loaded"], 16)
            sp.dma_start(xs[0][:], x_d[0]).then_inc(x_loaded[0], 16)
            sp.dma_start(wq_raw, wqT).then_inc(S["wq_loaded"], 16)
            sp.dma_start(xs[1][:], x_d[1]).then_inc(x_loaded[1], 16)
            sp.dma_start(w1_raw, w1T).then_inc(S["w1_loaded"], 16)
            sp.dma_start(w2_raw, w2T).then_inc(S["w2_loaded"], 16)
            sp.wait_ge(S["pick_ready"], 1)
            sp.dma_start(f32(k_stack[96:KROWS, :, :]), pick[:]).then_inc(S["pick_loaded"], 16)

            def part1(core, down, nxt):
                if down is not None:
                    i, u = down
                    sp.wait_ge(S["y_ready"], upto(down, 2, 2))
                    sp.dma_start(out_d[i * 2 + u], x2[u][:]).then_inc(out_stored[u], 16)

            def part2(tail, front, up, new_batch):
                if front is None:
                    return
                if tail is not None:
                    sp.wait_ge(S["st_ps"], upto(tail, NP, NP))
                if first(front):
                    sp.wait_ge(S["first_diag_ready"], KT)
                    stack_keys(sp, 0, "first_third_loaded")
                elif new_batch:
                    sp.wait_ge(S["k_diag_ready"], front[0] * 4 + 4)
                    for r in range(3):
                        stack_keys(sp, r, "k_stack_loaded")
                for r, s, ready in ((0, 0, "q_hi_ready"), (2, 0, "q_hi_ready"), (1, 1, "q_lo_ready")):
                    sp.wait_ge(S[ready], upto(front, KT, KT))
                    for g in range(QPT):
                        sp.dma_start(f32(q_stack_v[32 * r:32 * r + 32, :, g, :]), f32(qt[s][32 * g:32 * g + 32, :, :])
                                     ).then_inc(S["q_stack_loaded"], 16)
                i, u = step(front, 1)
                if tail is not None and not (isinstance(i, int) and i * 2 + u >= NC):
                    sp.wait_ge(S["x2_ready"], upto(tail, 2, 2))
                    sp.dma_start(xs[u][:], x_d[i * 2 + u]).then_inc(x_loaded[u], 16)
                sp.wait_ge(S["mt_ready"], upto(front, 1, 1))
                sp.dma_start(f32(q_stack[96:KROWS, :, :]),
                             f32(neg_max_t[:]).unsqueeze(1).broadcast_to([H, NP, C])
                             ).then_inc(S["q_stack_loaded"], 16)

            part2(None, FIRST, None, True)
            phases(sp, part1, part2)
            for u in range(2):
                sp.wait_ge(out_stored[u], 16 * (NC // 2))

        @block.gpsimd
        def _(pool):
            pool.memset(ident[:], 0.0).then_inc(S["ident_zeroed"], 1)
            pool.memset(head_mask[:], 1.0).then_inc(S["mask_set"], 1)
            pool.memset(pick[:], 0.0).then_inc(S["pick_zeroed"], 1)
            pool.memset(neg_half[:], -0.5).then_inc(S["half_set"], 1)
            pool.memset(eps[:], EPS).then_inc(S["half_set"], 1)
            pool.memset(v_ones[:], 1.0).then_inc(S["v_set"], 1)
            pool.wait_ge(S["ident_zeroed"], 1)
            pool.affine_select(out=ident[:], in_=ident[:], compare_op=ALU.not_equal, fill=1.0, base=0,
                               pattern=[[-1, P]], channel_multiplier=1).then_inc(S["ident_ready"], 1)
            pool.wait_ge(S["mask_set"], 1)
            pool.affine_select(out=head_mask[:], in_=head_mask[:], compare_op=ALU.is_ge, fill=0.0, base=0,
                               pattern=[[-HD, HPT]], channel_multiplier=1).then_inc(S["mask_low"], 1)
            pool.wait_ge(S["mask_low"], 1)
            pool.affine_select(out=head_mask[:], in_=head_mask[:], compare_op=ALU.is_ge, fill=0.0,
                               base=HD - 1, pattern=[[HD, HPT]], channel_multiplier=-1
                               ).then_inc(S["mask_ready"], 1)
            pool.wait_ge(S["pick_zeroed"], 1)
            pool.affine_select(out=pick[:], in_=pick[:], compare_op=ALU.not_equal, fill=1.0, base=0,
                               pattern=[[-1, H], [0, NK]], channel_multiplier=1).then_inc(S["pick_ready"], 1)

            pool.wait_ge(S["half_set"], 2)
            pool.wait_ge(S["ctx_mv"], B)
            pool.tensor_scalar(var_eps[0:NK, :], ctx_mv[:, :, 1], EPS, None, ALU.add).then_inc(S["ctx_var"], 1)
            pool.wait_ge(S["ctx_var"], 1)
            pool.tensor_tensor(ctx_rstd[:], var_eps[0:NK, :], neg_half[0:NK, :], ALU.pow
                               ).then_inc(S["ctx_rstd"], 1)

            def norm(c):
                pool.wait_ge(S["mv_ready"], upto(c, QT, QT))
                pool.tensor_tensor(var_eps[:], mv[:, :, 1], eps[:], ALU.add).then_inc(S["var_ready"], 1)
                pool.wait_ge(S["var_ready"], upto(c, 1, 1))
                pool.tensor_tensor(rstd[:], var_eps[:], neg_half[:], ALU.pow).then_inc(S["rstd_ready"], 1)

            def add_bo(c):
                pool.wait_ge(S["xn_ready"], upto(c, QT, QT))
                _, u = c
                pool.tensor_tensor(xs[u][:], xs[u][:], bo_row[:].unsqueeze(1).broadcast_to([P, QT, D]),
                                   ALU.add).then_inc(S["xbo_ready"], 1)

            def lo(dst, raw, hi, ready, done):
                pool.wait_ge(S[ready], 1)
                pool.tensor_tensor(dst, raw, hi, ALU.subtract).then_inc(S[done], 1)

            def spread_keys(s, b):
                for t in range(KT):
                    kd = f32(k_split[s][:, t, bass.ds(b * NK, NK)])
                    pool.tensor_tensor(k_diag[s][:, t, :, :], kd.unsqueeze(1).broadcast_to([P, HPT, NK]),
                                       head_mask[:].unsqueeze(2).broadcast_to([P, HPT, NK]), ALU.mult
                                       ).then_inc(S["k_diag_ready"], 2 if isinstance(b, int) and b == 0 else 1)

            pool.wait_ge(S["ctx_rstd"], 1)
            norm(FIRST)
            pool.wait_ge(S["mask_ready"], 1)
            pool.wait_ge(S["kd_lo_ready"], KT)
            spread_keys(1, 0)
            pool.wait_ge(S["first_diag_ready"], KT)
            stack_keys(pool, 1, "first_k_loaded")
            lo(wo[1][:], wo_raw, f32(wo[0][:]), "wo_hi_ready", "wo_lo_ready")
            pool.wait_ge(S["k_diag_ready"], 4)
            stack_keys(pool, 2, "first_k_loaded")
            pool.wait_ge(S["rows_loaded"], 32)
            norm((0, 1))
            add_bo(FIRST)
            lo(w1[1][:], w1_raw, f32(w1[0][:]), "w1_hi_ready", "w1_lo_ready")
            lo(w2[1][:], w2_raw, f32(w2[0][:]), "w2_hi_ready", "w2_lo_ready")
            add_bo((0, 1))

            def part1(core, down, nxt):
                if nxt is not None and not (isinstance(nxt[0], int) and nxt[0] == 0):
                    norm(nxt)
                    add_bo(nxt)
                if nxt is not None and nxt[1] == 0:
                    pool.wait_ge(S["s_ps"], upto(core, QT * KT, QT * KT))
                    if isinstance(nxt[0], int) and nxt[0] == 1:
                        pool.wait_ge(S["first_k_loaded"], 2 * QPT * 16)
                        pool.wait_ge(S["first_third_loaded"], QPT * 16)
                    else:
                        pool.wait_ge(S["k_stack_loaded"], (nxt[0] - 1) * (K_DMAS * 16))
                    spread_keys(0, nxt[0])
                    spread_keys(1, nxt[0])

            def part2(tail, front, up, new_batch):
                if tail is not None:
                    _, u = tail
                    pool.wait_ge(S["x2t_ps"], upto(tail, KT, KT))
                    pool.tensor_tensor(x2[u][:], x2[u][:], b2_row[:].unsqueeze(1).broadcast_to([P, QT, D]),
                                       ALU.add).then_inc(S["x2b_ready"], 1)

            phases(pool, part1, part2)

        @block.scalar
        def _(act):
            act.dma_start(par[:], params).then_inc(S["par_loaded"], 16)
            act.dma_start(wkv_raw, wkvT).then_inc(S["wkv_loaded"], 16)
            act.dma_start(wo_raw, woT).then_inc(S["wo_loaded"], 16)
            act.dma_start(bo_row[:], bo_d).then_inc(S["rows_loaded"], 16)
            act.dma_start(b2_row[:], b2_d).then_inc(S["rows_loaded"], 16)

            def place_values(b):
                act.activation(v_ones[:, :, 0, :],
                               v_all[:, bass.ds(b, 1), :].rearrange("k o (h d) -> k (o h) d", d=HD), ACT.Copy
                               ).then_inc(S["v_ones_ready"], 1)

            def turned_hi(c, banks):
                for k in range(KT):
                    act.wait_ge(S["xt_ps"], upto(c, KT, k + 1))
                    act.activation(xt[0][:, k, :], banks[k], ACT.Copy).then_inc(S["xt_hi_ready"], 1)

            def queries_hi(c, banks):
                for t in range(KT):
                    act.wait_ge(S["q_ps"], upto(c, KT, t + 1))
                    act.activation(qt[0][:, t, :], banks[t], ACT.Identity, bias=q_bias[:, t:t + 1]
                                   ).then_inc(S["q_hi_ready"], 1)

            turned_hi(FIRST, TURNED)
            for t in range(KT):
                act.wait_ge(S["kd_ps"], t + 1)
                act.activation(k_split[0][:, t, :], BANK[CD[t]][:, 0:B * NK], ACT.Copy
                               ).then_inc(S["kd_hi_ready"], 1)
            act.wait_ge(S["qb_ready"], 1)
            queries_hi(FIRST, PROJ)
            act.wait_ge(S["wo_loaded"], 16)
            act.activation(wo[0][:], wo_raw, ACT.Copy).then_inc(S["wo_hi_ready"], 1)
            for w, raw, name in ((w1, w1_raw, "w1"), (w2, w2_raw, "w2")):
                act.wait_ge(S[name + "_loaded"], 16)
                act.activation(w[0][:], raw, ACT.Copy).then_inc(S[name + "_hi_ready"], 1)
            for b in range(B):
                act.wait_ge(S["vd_ps"], b + 1)
                act.activation(v_all[:, b, :], BANK[AB[b % 2]][0:NK, 0:D], ACT.Copy).then_inc(S["v_ready"], 1)
            act.wait_ge(S["v_set"], 1)
            act.wait_ge(S["v_ready"], B)
            place_values(0)

            def part1(core, down, nxt):
                if core is None:
                    return
                if first(core):
                    act.wait_ge(S["wq_lo_ready"], KT)
                    act.wait_ge(S["wo_lo_ready"], 1)
                for g in range(NP):
                    act.wait_ge(S["st_ps"], upto(core, NP, g + 1))
                    if g >= PTR:
                        act.wait_ge(S["pv_ps"], upto(core, QT, (g - PTR) // 2 + 1))
                    act.activation(probs[0:NK, g % PTR, :, :], PAIR[g % 2][0:NK], ACT.Exp, scale=SCALE
                                   ).then_inc(S["exp_ready"], 1)
                    if early(nxt) and g == 3:
                        turned_hi(nxt, CD_BANKS)
                    if early(nxt) and g == 5:
                        queries_hi(nxt, CD_BANKS)

            def part2(tail, front, up, new_batch):
                def silu(*fs):
                    if up is None:
                        return
                    for f in fs:
                        if f == 0:
                            if first(up):
                                act.wait_ge(S["w1_lo_ready"], 1)
                                act.wait_ge(S["w2_lo_ready"], 1)
                            else:
                                act.wait_ge(S["h_lo_ready"], upto(step(up, -1), FT // 2, FT // 2))
                        act.wait_ge(S["h_ps"], upto(up, FT, f + 1))
                        act.activation(h_full[:, f, :], BANK[CD[f % 2]], ACT.Silu,
                                       bias=par[:, B1 + f:B1 + f + 1]).then_inc(S["h_full_ready"], 1)

                if front is not None and not early(front):
                    turned_hi(front, TURNED)
                silu(0, 1)
                if front is not None and not early(front):
                    queries_hi(front, PROJ)
                silu(2)
                if front is not None and new_batch:
                    act.wait_ge(S["pv_ps"], upto(tail, QT, QT))
                    place_values(front[0])
                if tail is not None:
                    for k in range(KT):
                        act.wait_ge(S["at_ps"], upto(tail, KT, k + 1))
                        act.activation(xt[0][:, k, :], BANK[AB[k]], ACT.Copy).then_inc(S["o_hi_ready"], 1)
                silu(3, 4, 5, 6, 7)
                if tail is not None:
                    for k in range(KT):
                        act.wait_ge(S["x2t_ps"], upto(tail, KT, k + 1))
                        act.activation(x2t[0][:, k, :], BANK[AB[k]], ACT.Copy).then_inc(S["x2_hi_ready"], 1)

            phases(act, part1, part2)

        @block.vector
        def _(dve):
            dve.wait_ge(S["ctx_loaded"], 16)
            for b in range(B):
                dve.bn_stats(stats[0:NK, b, :], ctx[:, b, :]).then_inc(S["ctx_stats"], 1)
            for b in range(B):
                dve.wait_ge(S["ctx_stats"], b + 1)
                dve.bn_aggr(ctx_mv[:, b, :], stats[0:NK, b, :]).then_inc(S["ctx_mv"], 1)
            def stats_of(c):
                i, u = c
                dve.wait_ge(x_loaded[u], i * 16 + 16)
                for q in range(QT):
                    dve.bn_stats(stats[:, q, :], xs[u][:, q, :]).then_inc(S["stats_ready"], 1)
                dve.wait_ge(S["stats_ready"], upto(c, QT, QT))

            def mean_var(c):
                for q in range(QT):
                    dve.bn_aggr(mv[:, q, :], stats[:, q, :]).then_inc(S["mv_ready"], 1)

            def normalise(c):
                _, u = c
                dve.wait_ge(S["rstd_ready"], upto(c, 1, 1))
                for q in range(QT):
                    dve.tensor_scalar(xn[:, q, :], xs[u][:, q, :], mv[:, q, 0:1], rstd[:, q:q + 1],
                                      ALU.subtract, ALU.mult).then_inc(S["xn_ready"], 1)

            def turned_lo(c, banks, k):
                dve.wait_ge(S["xt_hi_ready"], upto(c, KT, k + 1))
                dve.tensor_tensor(xt[1][:, k, :], banks[k], f32(xt[0][:, k, :]), ALU.subtract
                                  ).then_inc(S["xt_lo_ready"], 1)

            def queries_lo(c, banks, t):
                dve.wait_ge(S["q_hi_ready"], upto(c, KT, t + 1))
                dve.scalar_tensor_tensor(out=qt[1][:, t, :], in0=banks[t], scalar=q_bias[:, t:t + 1],
                                         in1=f32(qt[0][:, t, :]), op0=ALU.add, op1=ALU.subtract
                                         ).then_inc(S["q_lo_ready"], 1)

            def find_max(c, q):
                for t in range(KT):
                    dve.wait_ge(S["s_ps"], upto(c, QT * KT, KT * q + t + 1))
                    dve.tensor_reduce(neg_max[:, q, HPT * t:HPT * t + HPT].rearrange("p (a h) -> p a h", a=2),
                                      PAIR[t][:, :, 0:HPT // 2 * NK].rearrange("p a (h k) -> p a h k", k=NK),
                                      AX.X, ALU.max, negate=True).then_inc(S["max_ready"], 1)

            def turned_max(c):
                dve.wait_ge(S["mt_ps"], upto(c, 1, 1))
                dve.tensor_copy(neg_max_t[:], TURNED[0][0:H, :]).then_inc(S["mt_ready"], 1)

            dve.wait_ge(S["ctx_mv"], B)
            stats_of(FIRST)
            mean_var(FIRST)
            dve.wait_ge(S["ctx_rstd"], 1)
            for b in range(B):
                dve.tensor_scalar(ctx[:, b, :], ctx[:, b, :], ctx_mv[:, b, 0:1], ctx_rstd[:, b:b + 1],
                                  ALU.subtract, ALU.mult).then_inc(S["ctx_normed"], 1)
            normalise(FIRST)
            dve.wait_ge(S["par_loaded"], 16)
            for k in range(KT):
                dve.wait_ge(S["ctx_ps"], k + 1)
                dve.tensor_scalar(ctx_t[:, k, :], BANK[AB[k]][:, 0:B * NK], par[:, GKV + k:GKV + k + 1],
                                  par[:, BKV + k:BKV + k + 1], ALU.mult, ALU.add).then_inc(S["ctx_t_ready"], 1)
            dve.wait_ge(S["wq_loaded"], 16)
            for k in range(KT):
                dve.tensor_scalar(wq[0][:, k, :], wq_raw[:, k, :], par[:, GQ + k:GQ + k + 1], None, ALU.mult
                                  ).then_inc(S["wq_hi_ready"], 1)
            for k in range(KT):
                dve.wait_ge(S["wq_hi_ready"], k + 1)
                dve.scalar_tensor_tensor(out=wq[1][:, k, :], in0=wq_raw[:, k, :], scalar=par[:, GQ + k:GQ + k + 1],
                                         in1=f32(wq[0][:, k, :]), op0=ALU.mult, op1=ALU.subtract
                                         ).then_inc(S["wq_lo_ready"], 1)
            for k in range(KT):
                turned_lo(FIRST, TURNED, k)
            dve.wait_ge(S["mask_ready"], 1)
            for t in range(KT):
                dve.wait_ge(S["kd_hi_ready"], t + 1)
                dve.tensor_tensor(k_split[1][:, t, :], BANK[CD[t]][:, 0:B * NK], f32(k_split[0][:, t, :]),
                                  ALU.subtract).then_inc(S["kd_lo_ready"], 1)
                kd = f32(k_split[0][:, t, 0:NK])
                dve.tensor_tensor(k_diag[0][:, t, :, :], kd.unsqueeze(1).broadcast_to([P, HPT, NK]),
                                  head_mask[:].unsqueeze(2).broadcast_to([P, HPT, NK]), ALU.mult
                                  ).then_inc(S["first_diag_ready"], 1)
            dve.wait_ge(S["qb_ps"], 1)
            dve.tensor_copy(q_bias[:], BANK["A"][:, 0:KT]).then_inc(S["qb_ready"], 1)
            for t in range(KT):
                queries_lo(FIRST, PROJ, t)
            for q in range(QT):
                find_max(FIRST, q)
            turned_max(FIRST)

            def split_h(c, g):
                if g == 0 and not first(c):
                    dve.wait_ge(S["y_ps"], upto(step(c, -1), 2, 2))
                t = slice(2 * g, 2 * g + 2)
                dve.wait_ge(S["h_full_ready"], upto(c, FT, 2 * g + 2))
                dve.tensor_copy(h[0][:, t, :], h_full[:, t, :]).then_inc(S["h_hi_ready"], 1)
                dve.wait_ge(S["h_hi_ready"], upto(c, FT // 2, g + 1))
                dve.tensor_tensor(h[1][:, t, :], h_full[:, t, :], f32(h[0][:, t, :]), ALU.subtract
                                  ).then_inc(S["h_lo_ready"], 1)

            def save_o(c, *js):
                if c is not None:
                    for j in js:
                        dve.wait_ge(S["pv_ps"], upto(c, QT, j + 1))
                        dve.tensor_copy(o_raw[:, j, :], BANK[AB[j % 2]]).then_inc(S["o_raw_ready"], 1)

            def part1(core, down, nxt):
                if nxt is not None:
                    stats_of(nxt)
                if down is not None:
                    split_h(down, 3)
                if nxt is not None:
                    mean_var(nxt)
                if early(nxt):
                    normalise(nxt)
                    for k in range(KT):
                        turned_lo(nxt, CD_BANKS, k)
                save_o(core, 0)
                if nxt is not None and not early(nxt):
                    normalise(nxt)
                save_o(core, 1)
                if early(nxt):
                    for t in range(KT):
                        queries_lo(nxt, CD_BANKS, t)
                if down is not None:
                    _, u = down
                    dve.wait_ge(S["x2b_ready"], upto(down, 1, 1))
                    for s in range(2):
                        dve.wait_ge(S["y_ps"], upto(down, 2, s + 1))
                        y = x2[u][:, 2 * s:2 * s + 2, :]
                        dve.tensor_tensor(y, BANK[CD[s]].rearrange("p (q d) -> p q d", q=2), y, ALU.add
                                          ).then_inc(S["y_ready"], 1)

            def part2(tail, front, up, new_batch):
                for k in range(KT):
                    save_o(tail, 2 + k)
                    if front is not None and not early(front):
                        turned_lo(front, TURNED, k)
                if tail is not None:
                    for q in range(QT):
                        dve.wait_ge(S["ot_ps"], upto(tail, QT, q + 1))
                        o_v = BANK[AB[q % 2]].rearrange("p (h e d) -> p h e d", h=H, e=2)
                        dve.reciprocal(rsum[:, q, :], o_v[:, :, 1, 0]).then_inc(S["rsum_ready"], 1)
                        dve.wait_ge(S["rsum_ready"], upto(tail, QT, q + 1))
                        dve.tensor_tensor(o_nat[:, q, :].rearrange("p (h d) -> p h d", h=H), o_v[:, :, 0, :],
                                          rsum[:, q, :].unsqueeze(2).broadcast_to([P, H, HD]), ALU.mult
                                          ).then_inc(S["o_nat_ready"], 1)
                if up is not None:
                    split_h(up, 0)
                if front is not None:
                    if early(front):
                        find_max(front, 0)
                    else:
                        for t in range(KT):
                            queries_lo(front, PROJ, t)
                if tail is not None:
                    for k in range(KT):
                        dve.wait_ge(S["o_hi_ready"], upto(tail, KT, k + 1))
                        dve.tensor_tensor(xt[1][:, k, :], BANK[AB[k]], f32(xt[0][:, k, :]), ALU.subtract
                                          ).then_inc(S["o_lo_ready"], 1)
                if front is not None:
                    find_max(front, 1 if early(front) else 0)
                if up is not None:
                    split_h(up, 1)
                if tail is not None:
                    i, u = tail
                    if not (isinstance(i, int) and i == 0):
                        dve.wait_ge(out_stored[u], i * 16)
                    dve.wait_ge(S["xbo_ready"], upto(tail, 1, 1))
                    for s in range(2):
                        dve.wait_ge(S["op_ps"], upto(tail, 2, s + 1))
                        q = slice(2 * s, 2 * s + 2)
                        dve.tensor_tensor(x2[u][:, q, :], BANK[AB[s]].rearrange("p (q d) -> p q d", q=2),
                                          xs[u][:, q, :], ALU.add).then_inc(S["x2_ready"], 1)
                if front is not None:
                    for q in range(2 if early(front) else 1, QT):
                        find_max(front, q)
                    turned_max(front)
                if up is not None:
                    split_h(up, 2)
                if tail is not None:
                    for k in range(KT):
                        dve.wait_ge(S["x2_hi_ready"], upto(tail, KT, k + 1))
                        dve.tensor_tensor(x2t[1][:, k, :], BANK[AB[k]], f32(x2t[0][:, k, :]), ALU.subtract
                                          ).then_inc(S["x2_lo_ready"], 1)

            phases(dve, part1, part2)

        @block.tensor
        def _(pe):
            def turn(dst, src, n=P):
                return pe.transpose(dst, src, ident[0:n, 0:n])

            pe.wait_ge(S["ident_ready"], 1)
            for k in range(KT):
                for b in range(B):
                    pe.wait_ge(S["ctx_normed"], b + 1)
                    last = turn(BANK[AB[k]][:, b * NK:(b + 1) * NK], ctx[:, b, k * P:(k + 1) * P], NK)
                last.then_inc(S["ctx_ps"], 1)

            def turn_x(c, banks, k):
                pe.wait_ge(S["xn_ready"], upto(c, QT, QT))
                for q in range(QT):
                    last = turn(banks[k][:, q * P:(q + 1) * P], xn[:, q, k * P:(k + 1) * P])
                last.then_inc(S["xt_ps"], 1)

            def project_q(c, banks):
                pe.wait_ge(S["xt_lo_ready"], upto(c, KT, KT))
                for t in range(KT):
                    for n, (w, a) in enumerate(SPLITS):
                        for k in range(KT):
                            last = pe.matmul(banks[t], wq[w][:, k, t * P:(t + 1) * P], xt[a][:, k, :],
                                             start=(n == 0 and k == 0), stop=(n == 2 and k == KT - 1))
                    last.then_inc(S["q_ps"], 1)

            def scores(c, q, new_batch):
                for t in range(KT):
                    if q > 0:
                        pe.wait_ge(S["max_ready"], upto(c, QT * KT, KT * (q - 1) + t + 1))
                    else:
                        pe.wait_ge(S["q_lo_ready"], upto(c, KT, t + 1))
                        if new_batch:
                            if first(c):
                                pe.wait_ge(S["first_diag_ready"], t + 1)
                            else:
                                pe.wait_ge(S["k_diag_ready"], c[0] * 4 + t + 1)
                    for a in range(2):
                        last = pe.matmul(PAIR[t][:, a, 0:HPT // 2 * NK], qt[0][:, t, q * P:(q + 1) * P],
                                         k_diag[0][:, t, HPT // 2 * a:HPT // 2 * (a + 1), :],
                                         start=True, stop=True)
                    last.then_inc(S["s_ps"], 1)

            def turn_max(c):
                pe.wait_ge(S["max_ready"], upto(c, QT * KT, QT * KT))
                for q in range(QT):
                    last = turn(TURNED[0][0:H, q * P:(q + 1) * P], neg_max[:, q, :])
                last.then_inc(S["mt_ps"], 1)

            for k in range(KT):
                turn_x(FIRST, TURNED, k)
            pe.wait_ge(S["ctx_t_ready"], KT)
            pe.wait_ge(S["wkv_loaded"], 16)
            for t in range(KT):
                for k in range(KT):
                    last = pe.matmul(BANK[CD[t]][:, 0:B * NK], wkv_raw[:, k, t * P:(t + 1) * P], ctx_t[:, k, :],
                                     start=(k == 0), stop=(k == KT - 1))
                last.then_inc(S["kd_ps"], 1)
            pe.wait_ge(S["wq_loaded"], 16)
            pe.wait_ge(S["par_loaded"], 16)
            for t in range(KT):
                for k in range(KT):
                    last = pe.matmul(BANK["A"][:, t:t + 1], wq_raw[:, k, t * P:(t + 1) * P],
                                     par[:, BQ + k:BQ + k + 1], start=(k == 0), stop=(k == KT - 1))
            last.then_inc(S["qb_ps"], 1)
            pe.wait_ge(S["wq_lo_ready"], KT)
            project_q(FIRST, PROJ)
            pe.wait_ge(S["qb_ready"], 1)

            def project_v(b):
                if b >= 2:
                    pe.wait_ge(S["v_ready"], b - 1)
                for k in range(KT):
                    last = pe.matmul(BANK[AB[b % 2]][0:NK, 0:D], ctx_t[:, k, b * NK:(b + 1) * NK],
                                     wkv_raw[:, k, D:2 * D], start=(k == 0), stop=(k == KT - 1))
                last.then_inc(S["vd_ps"], 1)

            for q in range(QT):
                scores(FIRST, q, True)
                if q in (1, 2):
                    project_v(q - 1)
            turn_max(FIRST)
            project_v(2)
            project_v(3)

            def values(core, j):
                if j == 0 and core[1] == 0:
                    pe.wait_ge(S["v_ones_ready"], core[0] + 1)
                if j == 0 and not first(core):
                    pe.wait_ge(S["x2_lo_ready"], upto(step(core, -1), KT, KT))
                if j >= 2:
                    pe.wait_ge(S["o_raw_ready"], upto(core, QT, j - 1))
                pe.wait_ge(S["exp_ready"], upto(core, NP, 2 * j + 2))
                for n in range(4):
                    last = pe.matmul(BANK[AB[j % 2]][32 * n:32 * n + 32, :],
                                     v_ones[:, 4 * j + n, :, :].rearrange("k e d -> k (e d)"),
                                     probs[0:NK, (2 * j + n // 2) % PTR, n % 2, :], start=True, stop=True,
                                     tile_position=(0, 32 * n))
                last.then_inc(S["pv_ps"], 1)

            def part1(core, down, nxt):
                def down_tile(f):
                    if down is None:
                        return
                    if f == 0:
                        pe.wait_ge(S["h_full_ready"], upto(down, FT, FT))
                        if first(down):
                            pe.wait_ge(S["w2_lo_ready"], 1)
                    if f % 2 == 0:
                        pe.wait_ge(S["h_lo_ready"], upto(down, FT // 2, f // 2 + 1))
                    for s in range(2):
                        for q in range(2):
                            for n, (a, w) in enumerate(SPLITS):
                                last = pe.matmul(BANK[CD[s]][:, q * D:(q + 1) * D],
                                                 h[a][:, f, (2 * s + q) * P:(2 * s + q + 1) * P], w2[w][:, f, :],
                                                 start=(f == 0 and q == 0 and n == 0), stop=(f == FT - 1 and n == 2),
                                                 skip_group_check=True)
                        if f == FT - 1:
                            last.then_inc(S["y_ps"], 1)

                down_tile(0)
                down_tile(1)
                down_tile(2)
                down_beside = {0: 3, 1: 4, 2: 5, 4: 6, 6: 7}
                for g in range(NP):
                    if core is not None:
                        if g == 0:
                            pe.wait_ge(S["q_stack_loaded"], upto(core, Q_DMAS * 16, Q_DMAS * 16))
                            if first(core):
                                pe.wait_ge(S["pick_loaded"], 16)
                                pe.wait_ge(S["first_k_loaded"], 2 * QPT * 16)
                                pe.wait_ge(S["first_third_loaded"], QPT * 16)
                            elif core[1] == 0:
                                pe.wait_ge(S["k_stack_loaded"], core[0] * (K_DMAS * 16))
                        if g >= 2:
                            pe.wait_ge(S["exp_ready"], upto(core, NP, g - 1))
                        for e in range(2):
                            last = pe.matmul(PAIR[g % 2][0:NK, e, :], k_stack[:, 2 * g + e, :], q_stack[:, g, :],
                                             start=True, stop=True)
                        last.then_inc(S["st_ps"], 1)
                    if early(nxt) and g == 3:
                        for k in range(KT):
                            turn_x(nxt, CD_BANKS, k)
                    if early(nxt) and g == 5:
                        project_q(nxt, CD_BANKS)
                    if g in down_beside:
                        down_tile(down_beside[g])
                    if core is not None and g % 2 == 1 and g >= 3:
                        values(core, (g - 3) // 2)

            def part2(tail, front, up, new_batch):
                def up_tiles(*fs):
                    if up is None:
                        return
                    for f in fs:
                        if f == 0:
                            pe.wait_ge(S["x2_lo_ready"], upto(up, KT, KT))
                            if first(up):
                                pe.wait_ge(S["w1_lo_ready"], 1)
                        if f < 2:
                            if first(up):
                                pe.wait_ge(S["q_lo_ready"], upto((1, 0), KT, KT))
                            else:
                                pe.wait_ge(S["y_ready"], upto(step(up, -1), 2, f + 1))
                        else:
                            pe.wait_ge(S["h_full_ready"], upto(up, FT, f - 1))
                        for n, (w, a) in enumerate(SPLITS):
                            for k in range(KT):
                                last = pe.matmul(BANK[CD[f % 2]], w1[w][:, k, f * P:(f + 1) * P], x2t[a][:, k, :],
                                                 start=(n == 0 and k == 0), stop=(n == 2 and k == KT - 1))
                        last.then_inc(S["h_ps"], 1)

                def turn_o(*qs):
                    if tail is None:
                        return
                    for q in qs:
                        if q == 0:
                            pe.wait_ge(S["o_raw_ready"], upto(tail, QT, QT))
                        if q >= 2:
                            pe.wait_ge(S["o_nat_ready"], upto(tail, QT, q - 1))
                        for j in range(QT):
                            last = turn(BANK[AB[q % 2]][:, j * P:(j + 1) * P], o_raw[:, j, q * P:(q + 1) * P])
                        last.then_inc(S["ot_ps"], 1)

                def front_scores(*qs):
                    if front is not None:
                        for q in qs:
                            scores(front, q, new_batch)

                turned = front is None or early(front)
                if not turned:
                    pe.wait_ge(S["exp_ready"], upto(tail, NP, NP - 1))
                    turn_x(front, TURNED, 0)
                if tail is not None:
                    values(tail, 3)
                if not turned:
                    pe.wait_ge(S["exp_ready"], upto(tail, NP, NP))
                    turn_x(front, TURNED, 1)
                up_tiles(0)
                turn_o(0, 1)
                up_tiles(1)
                if turned:
                    front_scores(0)
                turn_o(2, 3)
                if not turned:
                    project_q(front, PROJ)
                up_tiles(2)
                if tail is not None:
                    pe.wait_ge(S["o_nat_ready"], upto(tail, QT, QT))
                    for k in range(KT):
                        for q in range(QT):
                            last = turn(BANK[AB[k]][:, q * P:(q + 1) * P], o_nat[:, q, k * P:(k + 1) * P])
                        last.then_inc(S["at_ps"], 1)
                up_tiles(3)
                front_scores(1 if turned else 0)
                if tail is not None:
                    if first(tail):
                        pe.wait_ge(S["wo_lo_ready"], 1)
                    pe.wait_ge(S["o_lo_ready"], upto(tail, KT, KT))
                    for s in range(2):
                        for q in range(2):
                            m = 0
                            for a, w in SPLITS:
                                for k in range(KT):
                                    last = pe.matmul(BANK[AB[s]][:, q * D:(q + 1) * D],
                                                     xt[a][:, k, (2 * s + q) * P:(2 * s + q + 1) * P], wo[w][:, k, :],
                                                     start=(m == 0), stop=(m == 3 * KT - 1))
                                    m += 1
                        last.then_inc(S["op_ps"], 1)
                up_tiles(4)
                if not turned:
                    front_scores(1)
                up_tiles(5)
                front_scores(2)
                up_tiles(6)
                front_scores(3)
                up_tiles(7)
                if front is not None:
                    turn_max(front)
                if tail is not None:
                    pe.wait_ge(S["x2_ready"], upto(tail, 2, 2))
                    _, u = tail
                    for k in range(KT):
                        for q in range(QT):
                            last = turn(BANK[AB[k]][:, q * P:(q + 1) * P], x2[u][:, q, k * P:(k + 1) * P])
                        last.then_inc(S["x2t_ps"], 1)

            phases(pe, part1, part2)


def kernel(**inputs):
    import numpy as np
    import concourse.bacc as bacc
    from concourse.bass_utils import run_bass_kernel_spmd as run

    a = {k.replace("L0_xattn_", ""): np.asarray(v) for k, v in inputs.items()}

    def by_rows(w):
        return np.ascontiguousarray(w.T.reshape(-1, P, w.shape[0]).transpose(1, 0, 2))

    def columns(v):
        return v.reshape(-1, P).T

    arrays = {
        "x": a["x"], "ctx": a["ctx_1024"],
        "wqT": by_rows(a["Wq"]), "wkvT": by_rows(a["Wkv"]), "woT": by_rows(a["Wo"]),
        "w1T": by_rows(a["W1"]), "w2T": by_rows(a["W2"]),
        "params": np.concatenate([columns(a[n]) for n in ("ln_q_g", "ln_q_b", "ln_kv_g", "ln_kv_b", "b1")], axis=1),
        "bo": np.broadcast_to(a["bo"], (P, D)), "b2": np.broadcast_to(a["b2"], (P, D)),
    }
    arrays = {f"in_{k}": np.ascontiguousarray(v) for k, v in arrays.items()}
    nc = bacc.Bacc("TRN2", target_bir_lowering=False, num_devices=1)
    args = [nc.dram_tensor(k, v.shape, mybir.dt.from_np(v.dtype), kind="ExternalInput").ap()
            for k, v in arrays.items()]
    out = nc.dram_tensor("out", (B, NQ, D), F32, kind="ExternalOutput").ap()
    build(nc, *args, out)
    r = run(nc, [arrays], core_ids=[0])
    return r.results[0]["out"]
```

```python
from contextlib import ExitStack

import concourse.bass as bass
from concourse import mybir

F32 = mybir.dt.float32
F32R = mybir.dt.float32r
ALU = mybir.AluOpType
ACT = mybir.ActivationFunctionType
AX = mybir.AxisListType

P = 128
B, NQ, NK, D = 4, 1024, 77, 256
H = 16
HD = D // H
DFF = 4 * D
C = 512
QT = C // P
KT = D // P
FT = DFF // P
NC = B * NQ // C
CPB = NQ // C
HPT = P // HD
NP = H // 2
QPT = P // 32
PTR = 4
KROWS = 96 + H
SCALE = HD ** -0.5
EPS = 1e-5
GQ, BQ, GKV, BKV, B1 = 0, KT, 2 * KT, 3 * KT, 4 * KT
NPAR = 4 * KT + FT


def step(c, d):
    i, u = c
    u += d
    return i + u // 2, u % 2


def first(c):
    return isinstance(c[0], int) and c == (0, 0)


def upto(c, n, k=0):
    i, u = c
    return i * (2 * n) + (n * u + k)


def build(nc, x, ctx_in, wqT, wkvT, woT, w1T, w2T, params, bo_d, b2_d, out):
    x_d = x.rearrange("b (h q p) d -> (b h) p q d", q=QT, p=P)
    out_d = out.rearrange("b (h q p) d -> (b h) p q d", q=QT, p=P)

    es = ExitStack()
    with es:
        def sb(name, shape, dt=F32):
            return es.enter_context(nc.sbuf_tensor(name, shape, dt))

        def sem(name):
            return es.enter_context(nc.semaphore(name))

        wq = [sb(f"wq_{s}", [P, KT, D], F32R) for s in ("hi", "lo")]
        wo = [sb(f"wo_{s}", [P, KT, D], F32R) for s in ("hi", "lo")]
        w1 = [sb(f"w1_{s}", [P, KT, DFF], F32R) for s in ("hi", "lo")]
        w2 = [sb(f"w2_{s}", [P, FT, D], F32R) for s in ("hi", "lo")]
        par = sb("par", [P, NPAR])
        q_bias = sb("q_bias", [P, KT])
        bo_row = sb("bo_row", [P, D])
        b2_row = sb("b2_row", [P, D])
        ident = sb("ident", [P, P], F32R)
        head_mask = sb("head_mask", [P, HPT])
        pick = sb("pick", [H, H, NK])
        neg_half = sb("neg_half", [P, QT])
        eps = sb("eps", [P, QT])
        k_split = [sb(f"k_{s}", [P, KT, B * NK], F32R) for s in ("hi", "lo")]
        k_diag = [sb(f"k_diag_{s}", [P, KT, HPT, NK], F32R) for s in ("hi", "lo")]
        k_stack = sb("k_stack", [KROWS, H, NK], F32R)
        v_all = sb("v_all", [NK, B, D])
        v_ones = sb("v_ones", [NK, H, 2, HD])
        xs = [sb(f"x_{u}", [P, QT, D]) for u in range(2)]
        stats = sb("stats", [P, QT, 6])
        mv = sb("mv", [P, QT, 2])
        var_eps = sb("var_eps", [P, QT])
        rstd = sb("rstd", [P, QT])
        ctx_mv = sb("ctx_mv", [NK, B, 2])
        ctx_rstd = sb("ctx_rstd", [NK, B])
        xn = sb("xn", [P, QT, D])
        xt = [sb(f"xt_{s}", [P, KT, C], F32R) for s in ("hi", "lo")]
        qt = [sb(f"qt_{s}", [P, KT, C], F32R) for s in ("hi", "lo")]
        q_stack = sb("q_stack", [KROWS, NP, C], F32R)
        neg_max = sb("neg_max", [P, QT, H], F32R)
        neg_max_t = sb("neg_max_t", [H, C], F32R)
        probs = sb("probs", [P, PTR, 2, C])
        o_raw = sb("o_raw", [P, QT, C])
        rsum = sb("rsum", [P, QT, H])
        o_nat = xn
        x2 = [sb(f"x2_{u}", [P, QT, D]) for u in range(2)]
        x2t = [sb(f"x2t_{s}", [P, KT, C], F32R) for s in ("hi", "lo")]
        h_full = sb("h_full", [P, FT, C])
        h = [sb(f"h_{s}", [P, FT, C], F32R) for s in ("hi", "lo")]
        q_stack_v = q_stack[:, :, :].rearrange("p (t g) n -> p t g n", t=KT)
        k_stack_v = k_stack[:, :, :].rearrange("p (t g e) k -> p t g (e k)", t=KT, e=2)
        k_diag_v = [kd[:, :, :, :].rearrange("p t (g e) k -> p t g (e k)", e=2) for kd in k_diag]
        w1_raw = h_full[:, 0:4, :].rearrange("p f n -> p (f n)").rearrange("p (k n) -> p k n", k=KT)
        w2_raw = h_full[:, 4:8, :].rearrange("p f n -> p (f n)").rearrange("p (f n) -> p f n", f=FT)
        pv_flat = probs[:, :, :, :].rearrange("p a b n -> p (a b n)")
        wkv_raw = pv_flat[:, 0:1024].rearrange("p (k n) -> p k n", k=KT)
        wq_raw = pv_flat[:, 1024:1536].rearrange("p (k n) -> p k n", k=KT)
        wo_raw = pv_flat[:, 1536:2048].rearrange("p (k n) -> p k n", k=KT)
        or_flat = o_raw[:, :, :].rearrange("p a n -> p (a n)")
        ctx = or_flat[0:NK, 0:B * D].rearrange("p (b n) -> p b n", b=B)
        ctx_t = or_flat[:, B * D:B * D + KT * B * NK].rearrange("p (k n) -> p k n", k=KT)

        ps = es.enter_context(nc.psum_tensor("ps", [P, 8, 512], F32))
        PAIR = [ps[:, 0:2, :], ps[:, 2:4, :]]
        BANK = {"A": ps[:, 4, :], "B": ps[:, 5, :], "C": ps[:, 6, :], "D": ps[:, 7, :]}
        AB, CD = "AB", "CD"
        CD_BANKS = [BANK["C"], BANK["D"]]
        TURNED = [PAIR[0][:, 0, :], PAIR[1][:, 0, :]]
        PROJ = [PAIR[0][:, 1, :], PAIR[1][:, 1, :]]

        names = """ctx_loaded wkv_loaded wq_loaded wo_loaded w1_loaded w2_loaded par_loaded rows_loaded
            ident_zeroed ident_ready mask_set mask_low mask_ready pick_zeroed pick_ready pick_loaded half_set
            v_set ctx_stats ctx_mv ctx_var ctx_rstd ctx_normed ctx_ps ctx_t_ready
            kd_ps kd_hi_ready kd_lo_ready vd_ps v_ready qb_ps qb_ready wq_hi_ready wq_lo_ready
            wo_hi_ready wo_lo_ready w1_hi_ready w1_lo_ready w2_hi_ready w2_lo_ready
            first_diag_hi_ready first_keys_by_pool first_keys_by_sp k_diag_ready k_stack_loaded v_ones_ready
            stats_ready mv_ready var_ready rstd_ready xn_ready xbo_ready
            xt_ps xt_hi_ready xt_lo_ready q_ps q_hi_ready q_lo_ready q_stack_loaded
            s_ps max_ready mt_ps mt_ready st_ps exp_ready pv_ps o_raw_ready
            ot_ps rsum_ready o_nat_ready at_ps o_hi_ready o_lo_ready op_ps x2_ready
            x2t_ps x2_hi_ready x2_lo_ready x2b_ready h_ps h_full_ready h_hi_ready h_lo_ready
            y_ps y_ready""".split()
        S = {n: sem(n) for n in names}
        x_loaded = [sem(f"x_loaded_{u}") for u in range(2)]
        out_stored = [sem(f"out_stored_{u}") for u in range(2)]

        block = es.enter_context(nc.Block())
        FIRST, SECOND = (0, 0), (0, 1)
        Q_DMAS, K_DMAS = 3 * QPT + 1, 3 * QPT
        SPLITS = ((0, 0), (0, 1), (1, 0))

        def f32(ap):
            return ap.bitcast(F32)

        def stack_keys(eng, r, loaded):
            for g in range(QPT):
                eng.dma_start(f32(k_stack_v[32 * r:32 * r + 32, :, g, :]),
                              f32(k_diag_v[r // 2][32 * g:32 * g + 32, :, g, :])
                              ).then_inc(S[loaded], 16)

        def second(c):
            return c is not None and isinstance(c[0], int) and c == SECOND

        def maxima_at(front, place):
            if front is None:
                return ()
            if second(front):
                return {"start": (0,), "half divided": (1,), "divided": (2,), "turned": (3,)}.get(place, ())
            return {"turned": (0,), "projected": (1,), "residual": (2,), "end": (3,)}.get(place, ())

        def phases(eng, part1, part2):
            def phase(c, p=None):
                core = c if p is None or p < NC else None
                down = step(c, -2) if p is None or p >= 2 else None
                nxt = step(c, 1) if p is None or p + 1 < NC else None
                up = step(c, -1) if p is None or 1 <= p <= NC else None
                part1(core, down, nxt)
                part2(core, nxt, up, c[1] == 1)

            for p in (0, 1):
                phase((0, p), p)
            with eng.Fori(1, 3) as i:
                for u in range(2):
                    phase((i, u))
            for p in range(6, NC + 2):
                phase((p // 2, p % 2), p)

        @block.sync
        def _(sp):
            sp.dma_start(ctx, ctx_in.rearrange("b k d -> k b d")).then_inc(S["ctx_loaded"], 16)
            sp.dma_start(xs[0][:], x_d[0]).then_inc(x_loaded[0], 16)
            sp.dma_start(wq_raw, wqT).then_inc(S["wq_loaded"], 16)
            sp.dma_start(xs[1][:], x_d[1]).then_inc(x_loaded[1], 16)
            sp.dma_start(w1_raw, w1T).then_inc(S["w1_loaded"], 16)
            sp.dma_start(w2_raw, w2T).then_inc(S["w2_loaded"], 16)
            sp.wait_ge(S["pick_ready"], 1)
            sp.dma_start(f32(k_stack[96:KROWS, :, :]), pick[:]).then_inc(S["pick_loaded"], 16)

            def part1(core, down, nxt):
                if down is not None:
                    i, u = down
                    if isinstance(i, int) and i * 2 + u == NC - 1:
                        for s in range(2):
                            q = slice(2 * s, 2 * s + 2)
                            sp.wait_ge(S["y_ready"], upto(down, 2, s + 1))
                            sp.dma_start(out_d[i * 2 + u][:, q, :], x2[u][:, q, :]).then_inc(out_stored[u], 16)
                    else:
                        sp.wait_ge(S["y_ready"], upto(down, 2, 2))
                        sp.dma_start(out_d[i * 2 + u], x2[u][:]).then_inc(out_stored[u], 16)

            def part2(tail, front, up, new_batch):
                if front is None:
                    return
                if tail is not None:
                    sp.wait_ge(S["st_ps"], upto(tail, NP, NP))
                if first(front):
                    sp.wait_ge(S["first_diag_hi_ready"], KT)
                    stack_keys(sp, 0, "first_keys_by_sp")
                elif new_batch:
                    sp.wait_ge(S["k_diag_ready"], front[0] * 4 + 4)
                    for r in range(3):
                        stack_keys(sp, r, "k_stack_loaded")
                for r, s, ready in ((0, 0, "q_hi_ready"), (2, 0, "q_hi_ready"), (1, 1, "q_lo_ready")):
                    sp.wait_ge(S[ready], upto(front, KT, KT))
                    for g in range(QPT):
                        sp.dma_start(f32(q_stack_v[32 * r:32 * r + 32, :, g, :]), f32(qt[s][32 * g:32 * g + 32, :, :])
                                     ).then_inc(S["q_stack_loaded"], 16)
                i, u = step(front, 1)
                if tail is not None and not (isinstance(i, int) and i * 2 + u >= NC):
                    sp.wait_ge(S["x2_ready"], upto(tail, 2, 2))
                    sp.dma_start(xs[u][:], x_d[i * 2 + u]).then_inc(x_loaded[u], 16)
                sp.wait_ge(S["mt_ready"], upto(front, 1, 1))
                sp.dma_start(f32(q_stack[96:KROWS, :, :]),
                             f32(neg_max_t[:]).unsqueeze(1).broadcast_to([H, NP, C])
                             ).then_inc(S["q_stack_loaded"], 16)

            part2(None, FIRST, None, True)
            phases(sp, part1, part2)
            sp.wait_ge(out_stored[0], 16 * (NC // 2))
            sp.wait_ge(out_stored[1], 16 * (NC // 2) + 16)

        @block.gpsimd
        def _(pool):
            pool.memset(f32(ident[:]), 0.0).then_inc(S["ident_zeroed"], 1)
            pool.memset(head_mask[:], 1.0).then_inc(S["mask_set"], 1)
            pool.memset(pick[:], 0.0).then_inc(S["pick_zeroed"], 1)
            pool.memset(neg_half[:], -0.5).then_inc(S["half_set"], 1)
            pool.memset(eps[:], EPS).then_inc(S["half_set"], 1)
            pool.memset(v_ones[:], 1.0).then_inc(S["v_set"], 1)
            pool.wait_ge(S["ident_zeroed"], 1)
            pool.affine_select(out=ident[:], in_=f32(ident[:]), compare_op=ALU.not_equal, fill=1.0, base=0,
                               pattern=[[-1, P]], channel_multiplier=1).then_inc(S["ident_ready"], 1)
            pool.wait_ge(S["mask_set"], 1)
            pool.affine_select(out=head_mask[:], in_=head_mask[:], compare_op=ALU.is_ge, fill=0.0, base=0,
                               pattern=[[-HD, HPT]], channel_multiplier=1).then_inc(S["mask_low"], 1)
            pool.wait_ge(S["mask_low"], 1)
            pool.affine_select(out=head_mask[:], in_=head_mask[:], compare_op=ALU.is_ge, fill=0.0,
                               base=HD - 1, pattern=[[HD, HPT]], channel_multiplier=-1
                               ).then_inc(S["mask_ready"], 1)
            pool.wait_ge(S["pick_zeroed"], 1)
            pool.affine_select(out=pick[:], in_=pick[:], compare_op=ALU.not_equal, fill=1.0, base=0,
                               pattern=[[-1, H], [0, NK]], channel_multiplier=1).then_inc(S["pick_ready"], 1)

            pool.wait_ge(S["half_set"], 2)
            pool.wait_ge(S["ctx_mv"], B)
            pool.tensor_scalar(var_eps[0:NK, :], ctx_mv[:, :, 1], EPS, None, ALU.add).then_inc(S["ctx_var"], 1)
            pool.wait_ge(S["ctx_var"], 1)
            pool.tensor_tensor(ctx_rstd[:], var_eps[0:NK, :], neg_half[0:NK, :], ALU.pow
                               ).then_inc(S["ctx_rstd"], 1)

            def norm(c):
                pool.wait_ge(S["mv_ready"], upto(c, QT, QT))
                pool.tensor_tensor(var_eps[:], mv[:, :, 1], eps[:], ALU.add).then_inc(S["var_ready"], 1)
                pool.wait_ge(S["var_ready"], upto(c, 1, 1))
                pool.tensor_tensor(rstd[:], var_eps[:], neg_half[:], ALU.pow).then_inc(S["rstd_ready"], 1)

            def add_bo(c):
                pool.wait_ge(S["xn_ready"], upto(c, QT, QT))
                _, u = c
                pool.tensor_tensor(xs[u][:], xs[u][:], bo_row[:].unsqueeze(1).broadcast_to([P, QT, D]),
                                   ALU.add).then_inc(S["xbo_ready"], 1)

            def lo(dst, raw, hi, ready, done):
                pool.wait_ge(S[ready], 1)
                pool.tensor_tensor(dst, raw, hi, ALU.subtract).then_inc(S[done], 1)

            def spread_keys(s, b):
                for t in range(KT):
                    kd = f32(k_split[s][:, t, bass.ds(b * NK, NK)])
                    pool.tensor_tensor(k_diag[s][:, t, :, :], kd.unsqueeze(1).broadcast_to([P, HPT, NK]),
                                       head_mask[:].unsqueeze(2).broadcast_to([P, HPT, NK]), ALU.mult
                                       ).then_inc(S["k_diag_ready"], 2 if isinstance(b, int) and b == 0 else 1)

            pool.wait_ge(S["ctx_rstd"], 1)
            norm(FIRST)
            norm(SECOND)
            pool.wait_ge(S["mask_ready"], 1)
            pool.wait_ge(S["kd_lo_ready"], KT)
            spread_keys(1, 0)
            pool.wait_ge(S["first_diag_hi_ready"], KT)
            stack_keys(pool, 1, "first_keys_by_pool")
            lo(wo[1][:], wo_raw, f32(wo[0][:]), "wo_hi_ready", "wo_lo_ready")
            pool.wait_ge(S["k_diag_ready"], 4)
            stack_keys(pool, 2, "first_keys_by_pool")
            pool.wait_ge(S["rows_loaded"], 32)
            add_bo(FIRST)
            lo(w1[1][:], w1_raw, f32(w1[0][:]), "w1_hi_ready", "w1_lo_ready")
            lo(w2[1][:], w2_raw, f32(w2[0][:]), "w2_hi_ready", "w2_lo_ready")
            add_bo(SECOND)

            def part1(core, down, nxt):
                if nxt is not None and not (isinstance(nxt[0], int) and nxt[0] == 0):
                    norm(nxt)
                    add_bo(nxt)
                if nxt is not None and nxt[1] == 0:
                    pool.wait_ge(S["s_ps"], upto(core, QT * KT, QT * KT))
                    if isinstance(nxt[0], int) and nxt[0] == 1:
                        pool.wait_ge(S["first_keys_by_pool"], 2 * QPT * 16)
                        pool.wait_ge(S["first_keys_by_sp"], QPT * 16)
                    else:
                        pool.wait_ge(S["k_stack_loaded"], (nxt[0] - 1) * (K_DMAS * 16))
                    spread_keys(0, nxt[0])
                    spread_keys(1, nxt[0])

            def part2(tail, front, up, new_batch):
                if tail is not None:
                    _, u = tail
                    pool.wait_ge(S["x2t_ps"], upto(tail, KT, KT))
                    pool.tensor_tensor(x2[u][:], x2[u][:], b2_row[:].unsqueeze(1).broadcast_to([P, QT, D]),
                                       ALU.add).then_inc(S["x2b_ready"], 1)

            phases(pool, part1, part2)

        @block.scalar
        def _(act):
            act.dma_start(par[:], params).then_inc(S["par_loaded"], 16)
            act.dma_start(wkv_raw, wkvT).then_inc(S["wkv_loaded"], 16)
            act.dma_start(wo_raw, woT).then_inc(S["wo_loaded"], 16)
            act.dma_start(bo_row[:], bo_d).then_inc(S["rows_loaded"], 16)
            act.dma_start(b2_row[:], b2_d).then_inc(S["rows_loaded"], 16)

            def place_values(b):
                act.activation(v_ones[:, :, 0, :],
                               v_all[:, bass.ds(b, 1), :].rearrange("k o (h d) -> k (o h) d", d=HD), ACT.Copy
                               ).then_inc(S["v_ones_ready"], 1)

            def turned_hi(c, banks):
                for k in range(KT):
                    act.wait_ge(S["xt_ps"], upto(c, KT, k + 1))
                    act.activation(xt[0][:, k, :], banks[k], ACT.Copy).then_inc(S["xt_hi_ready"], 1)

            def queries_hi(c, banks):
                for t in range(KT):
                    act.wait_ge(S["q_ps"], upto(c, KT, t + 1))
                    act.activation(qt[0][:, t, :], banks[t], ACT.Identity, bias=q_bias[:, t:t + 1]
                                   ).then_inc(S["q_hi_ready"], 1)

            act.wait_ge(S["par_loaded"], 16)
            act.wait_ge(S["wq_loaded"], 16)
            for k in range(KT):
                act.activation(wq[0][:, k, :], wq_raw[:, k, :], ACT.Copy, scale=par[:, GQ + k:GQ + k + 1]
                               ).then_inc(S["wq_hi_ready"], 1)
            for k in range(KT):
                act.wait_ge(S["ctx_ps"], k + 1)
                act.activation(ctx_t[:, k, :], BANK[AB[k]][:, 0:B * NK], ACT.Identity,
                               scale=par[:, GKV + k:GKV + k + 1], bias=par[:, BKV + k:BKV + k + 1]
                               ).then_inc(S["ctx_t_ready"], 1)
            turned_hi(FIRST, TURNED)
            for t in range(KT):
                act.wait_ge(S["kd_ps"], t + 1)
                act.activation(k_split[0][:, t, :], BANK[CD[t]][:, 0:B * NK], ACT.Copy
                               ).then_inc(S["kd_hi_ready"], 1)
            act.wait_ge(S["qb_ready"], 1)
            queries_hi(FIRST, PROJ)
            turned_hi(SECOND, CD_BANKS)
            act.wait_ge(S["wo_loaded"], 16)
            act.activation(wo[0][:], wo_raw, ACT.Copy).then_inc(S["wo_hi_ready"], 1)
            for w, raw, name in ((w1, w1_raw, "w1"), (w2, w2_raw, "w2")):
                act.wait_ge(S[name + "_loaded"], 16)
                act.activation(w[0][:], raw, ACT.Copy).then_inc(S[name + "_hi_ready"], 1)
            for b in range(B):
                act.wait_ge(S["vd_ps"], b + 1)
                act.activation(v_all[:, b, :], BANK[AB[b % 2]][0:NK, 0:D], ACT.Copy).then_inc(S["v_ready"], 1)
            act.wait_ge(S["v_set"], 1)
            act.wait_ge(S["v_ready"], B)
            place_values(0)

            def part1(core, down, nxt):
                if core is None:
                    return
                if first(core):
                    act.wait_ge(S["wq_lo_ready"], KT)
                    act.wait_ge(S["wo_lo_ready"], 1)
                for g in range(NP):
                    act.wait_ge(S["st_ps"], upto(core, NP, g + 1))
                    if g >= PTR:
                        act.wait_ge(S["pv_ps"], upto(core, QT, (g - PTR) // 2 + 1))
                    act.activation(probs[0:NK, g % PTR, :, :], PAIR[g % 2][0:NK], ACT.Exp, scale=SCALE
                                   ).then_inc(S["exp_ready"], 1)
                    if second(nxt) and g == 1:
                        queries_hi(nxt, CD_BANKS)

            def part2(tail, front, up, new_batch):
                def silu(*fs):
                    if up is None:
                        return
                    for f in fs:
                        if f == 0:
                            if first(up):
                                act.wait_ge(S["w1_lo_ready"], 1)
                                act.wait_ge(S["w2_lo_ready"], 1)
                            else:
                                act.wait_ge(S["h_lo_ready"], upto(step(up, -1), FT // 2, FT // 2))
                        act.wait_ge(S["h_ps"], upto(up, FT, f + 1))
                        act.activation(h_full[:, f, :], BANK[CD[f % 2]], ACT.Silu,
                                       bias=par[:, B1 + f:B1 + f + 1]).then_inc(S["h_full_ready"], 1)

                if front is not None and not second(front):
                    turned_hi(front, TURNED)
                silu(0, 1)
                if front is not None and not second(front):
                    queries_hi(front, PROJ)
                silu(2)
                if front is not None and new_batch:
                    act.wait_ge(S["pv_ps"], upto(tail, QT, QT))
                    place_values(front[0])
                if tail is not None:
                    for k in range(KT):
                        act.wait_ge(S["at_ps"], upto(tail, KT, k + 1))
                        act.activation(xt[0][:, k, :], BANK[AB[k]], ACT.Copy).then_inc(S["o_hi_ready"], 1)
                silu(3, 4, 5, 6, 7)
                if tail is not None:
                    for k in range(KT):
                        act.wait_ge(S["x2t_ps"], upto(tail, KT, k + 1))
                        act.activation(x2t[0][:, k, :], BANK[AB[k]], ACT.Copy).then_inc(S["x2_hi_ready"], 1)

            phases(act, part1, part2)

        @block.vector
        def _(dve):
            dve.wait_ge(S["ctx_loaded"], 16)
            for b in range(B):
                dve.bn_stats(stats[0:NK, b, :], ctx[:, b, :]).then_inc(S["ctx_stats"], 1)
            for b in range(B):
                dve.wait_ge(S["ctx_stats"], b + 1)
                dve.bn_aggr(ctx_mv[:, b, :], stats[0:NK, b, :]).then_inc(S["ctx_mv"], 1)
            def stats_of(c):
                i, u = c
                dve.wait_ge(x_loaded[u], i * 16 + 16)
                for q in range(QT):
                    dve.bn_stats(stats[:, q, :], xs[u][:, q, :]).then_inc(S["stats_ready"], 1)
                dve.wait_ge(S["stats_ready"], upto(c, QT, QT))

            def mean_var(c):
                for q in range(QT):
                    dve.bn_aggr(mv[:, q, :], stats[:, q, :]).then_inc(S["mv_ready"], 1)

            def normalise(c):
                _, u = c
                dve.wait_ge(S["rstd_ready"], upto(c, 1, 1))
                for q in range(QT):
                    dve.tensor_scalar(xn[:, q, :], xs[u][:, q, :], mv[:, q, 0:1], rstd[:, q:q + 1],
                                      ALU.subtract, ALU.mult).then_inc(S["xn_ready"], 1)

            def turned_lo(c, banks, k):
                dve.wait_ge(S["xt_hi_ready"], upto(c, KT, k + 1))
                dve.tensor_tensor(xt[1][:, k, :], banks[k], f32(xt[0][:, k, :]), ALU.subtract
                                  ).then_inc(S["xt_lo_ready"], 1)

            def queries_lo(c, banks, t):
                dve.wait_ge(S["q_hi_ready"], upto(c, KT, t + 1))
                dve.scalar_tensor_tensor(out=qt[1][:, t, :], in0=banks[t], scalar=q_bias[:, t:t + 1],
                                         in1=f32(qt[0][:, t, :]), op0=ALU.add, op1=ALU.subtract
                                         ).then_inc(S["q_lo_ready"], 1)

            def find_max(c, q):
                for t in range(KT):
                    dve.wait_ge(S["s_ps"], upto(c, QT * KT, KT * q + t + 1))
                    dve.tensor_reduce(neg_max[:, q, HPT * t:HPT * t + HPT].rearrange("p (a h) -> p a h", a=2),
                                      PAIR[t][:, :, 0:HPT // 2 * NK].rearrange("p a (h k) -> p a h k", k=NK),
                                      AX.X, ALU.max, negate=True).then_inc(S["max_ready"], 1)

            def turned_max(c):
                dve.wait_ge(S["mt_ps"], upto(c, 1, 1))
                dve.tensor_copy(neg_max_t[:], TURNED[0][0:H, :]).then_inc(S["mt_ready"], 1)

            dve.wait_ge(S["ctx_mv"], B)
            stats_of(FIRST)
            mean_var(FIRST)
            dve.wait_ge(S["ctx_rstd"], 1)
            for b in range(B):
                dve.tensor_scalar(ctx[:, b, :], ctx[:, b, :], ctx_mv[:, b, 0:1], ctx_rstd[:, b:b + 1],
                                  ALU.subtract, ALU.mult).then_inc(S["ctx_normed"], 1)
            normalise(FIRST)
            stats_of(SECOND)
            for k in range(KT):
                turned_lo(FIRST, TURNED, k)
            mean_var(SECOND)
            for k in range(KT):
                dve.wait_ge(S["wq_hi_ready"], k + 1)
                dve.scalar_tensor_tensor(out=wq[1][:, k, :], in0=wq_raw[:, k, :], scalar=par[:, GQ + k:GQ + k + 1],
                                         in1=f32(wq[0][:, k, :]), op0=ALU.mult, op1=ALU.subtract
                                         ).then_inc(S["wq_lo_ready"], 1)
            dve.wait_ge(S["mask_ready"], 1)
            for t in range(KT):
                dve.wait_ge(S["kd_hi_ready"], t + 1)
                dve.tensor_tensor(k_split[1][:, t, :], BANK[CD[t]][:, 0:B * NK], f32(k_split[0][:, t, :]),
                                  ALU.subtract).then_inc(S["kd_lo_ready"], 1)
                kd = f32(k_split[0][:, t, 0:NK])
                dve.tensor_tensor(k_diag[0][:, t, :, :], kd.unsqueeze(1).broadcast_to([P, HPT, NK]),
                                  head_mask[:].unsqueeze(2).broadcast_to([P, HPT, NK]), ALU.mult
                                  ).then_inc(S["first_diag_hi_ready"], 1)
            dve.wait_ge(S["qb_ps"], 1)
            dve.tensor_copy(q_bias[:], BANK["A"][:, 0:KT]).then_inc(S["qb_ready"], 1)
            normalise(SECOND)
            for t in range(KT):
                queries_lo(FIRST, PROJ, t)
            for q in range(QT):
                find_max(FIRST, q)
            turned_max(FIRST)
            for k in range(KT):
                turned_lo(SECOND, CD_BANKS, k)

            def split_h(c, g):
                if g == 0 and not first(c):
                    dve.wait_ge(S["y_ps"], upto(step(c, -1), 2, 2))
                t = slice(2 * g, 2 * g + 2)
                dve.wait_ge(S["h_full_ready"], upto(c, FT, 2 * g + 2))
                dve.tensor_copy(h[0][:, t, :], h_full[:, t, :]).then_inc(S["h_hi_ready"], 1)
                dve.wait_ge(S["h_hi_ready"], upto(c, FT // 2, g + 1))
                dve.tensor_tensor(h[1][:, t, :], h_full[:, t, :], f32(h[0][:, t, :]), ALU.subtract
                                  ).then_inc(S["h_lo_ready"], 1)

            def save_o(c, *js):
                if c is not None:
                    for j in js:
                        dve.wait_ge(S["pv_ps"], upto(c, QT, j + 1))
                        dve.tensor_copy(o_raw[:, j, :], BANK[AB[j % 2]]).then_inc(S["o_raw_ready"], 1)

            def part1(core, down, nxt):
                if nxt is not None and not second(nxt):
                    stats_of(nxt)
                if down is not None:
                    split_h(down, 3)
                if nxt is not None and not second(nxt):
                    mean_var(nxt)
                if second(nxt):
                    for t in range(KT):
                        queries_lo(nxt, CD_BANKS, t)
                save_o(core, 0)
                if nxt is not None and not second(nxt):
                    normalise(nxt)
                save_o(core, 1)
                if down is not None:
                    _, u = down
                    dve.wait_ge(S["x2b_ready"], upto(down, 1, 1))
                    for s in range(2):
                        dve.wait_ge(S["y_ps"], upto(down, 2, s + 1))
                        y = x2[u][:, 2 * s:2 * s + 2, :]
                        dve.tensor_tensor(y, BANK[CD[s]].rearrange("p (q d) -> p q d", q=2), y, ALU.add
                                          ).then_inc(S["y_ready"], 1)

            def part2(tail, front, up, new_batch):
                def maxima(place):
                    for q in maxima_at(front, place):
                        find_max(front, q)

                for k in range(KT):
                    save_o(tail, 2 + k)
                    if front is not None and not second(front):
                        turned_lo(front, TURNED, k)
                maxima("start")
                if tail is not None:
                    for q in range(QT):
                        dve.wait_ge(S["ot_ps"], upto(tail, QT, q + 1))
                        o_v = BANK[AB[q % 2]].rearrange("p (h e d) -> p h e d", h=H, e=2)
                        dve.reciprocal(rsum[:, q, :], o_v[:, :, 1, 0]).then_inc(S["rsum_ready"], 1)
                        dve.wait_ge(S["rsum_ready"], upto(tail, QT, q + 1))
                        dve.tensor_tensor(o_nat[:, q, :].rearrange("p (h d) -> p h d", h=H), o_v[:, :, 0, :],
                                          rsum[:, q, :].unsqueeze(2).broadcast_to([P, H, HD]), ALU.mult
                                          ).then_inc(S["o_nat_ready"], 1)
                        if q == 1:
                            maxima("half divided")
                maxima("divided")
                if up is not None:
                    split_h(up, 0)
                if front is not None and not second(front):
                    for t in range(KT):
                        queries_lo(front, PROJ, t)
                if tail is not None:
                    for k in range(KT):
                        dve.wait_ge(S["o_hi_ready"], upto(tail, KT, k + 1))
                        dve.tensor_tensor(xt[1][:, k, :], BANK[AB[k]], f32(xt[0][:, k, :]), ALU.subtract
                                          ).then_inc(S["o_lo_ready"], 1)
                maxima("turned")
                if up is not None:
                    split_h(up, 1)
                if tail is not None:
                    i, u = tail
                    if not (isinstance(i, int) and i == 0):
                        dve.wait_ge(out_stored[u], i * 16)
                    dve.wait_ge(S["xbo_ready"], upto(tail, 1, 1))
                    for s in range(2):
                        dve.wait_ge(S["op_ps"], upto(tail, 2, s + 1))
                        q = slice(2 * s, 2 * s + 2)
                        dve.tensor_tensor(x2[u][:, q, :], BANK[AB[s]].rearrange("p (q d) -> p q d", q=2),
                                          xs[u][:, q, :], ALU.add).then_inc(S["x2_ready"], 1)
                maxima("projected")
                maxima("residual")
                maxima("end")
                if front is not None:
                    turned_max(front)
                if up is not None:
                    split_h(up, 2)
                if tail is not None:
                    for k in range(KT):
                        dve.wait_ge(S["x2_hi_ready"], upto(tail, KT, k + 1))
                        dve.tensor_tensor(x2t[1][:, k, :], BANK[AB[k]], f32(x2t[0][:, k, :]), ALU.subtract
                                          ).then_inc(S["x2_lo_ready"], 1)

            phases(dve, part1, part2)

        @block.tensor
        def _(pe):
            def turn(dst, src, n=P):
                return pe.transpose(dst, src, f32(ident[0:n, 0:n]))

            pe.wait_ge(S["ident_ready"], 1)
            for k in range(KT):
                for b in range(B):
                    pe.wait_ge(S["ctx_normed"], b + 1)
                    last = turn(BANK[AB[k]][:, b * NK:(b + 1) * NK], ctx[:, b, k * P:(k + 1) * P], NK)
                last.then_inc(S["ctx_ps"], 1)

            def turn_x(c, banks, k):
                pe.wait_ge(S["xn_ready"], upto(c, QT, QT))
                for q in range(QT):
                    last = turn(banks[k][:, q * P:(q + 1) * P], xn[:, q, k * P:(k + 1) * P])
                last.then_inc(S["xt_ps"], 1)

            def project_q(c, banks):
                pe.wait_ge(S["xt_lo_ready"], upto(c, KT, KT))
                for t in range(KT):
                    for n, (w, a) in enumerate(SPLITS):
                        for k in range(KT):
                            last = pe.matmul(banks[t], wq[w][:, k, t * P:(t + 1) * P], xt[a][:, k, :],
                                             start=(n == 0 and k == 0), stop=(n == 2 and k == KT - 1))
                    last.then_inc(S["q_ps"], 1)

            def scores(c, q, new_batch):
                for t in range(KT):
                    if q > 0:
                        pe.wait_ge(S["max_ready"], upto(c, QT * KT, KT * (q - 1) + t + 1))
                    else:
                        pe.wait_ge(S["q_lo_ready"], upto(c, KT, t + 1))
                        if new_batch:
                            if first(c):
                                pe.wait_ge(S["first_diag_hi_ready"], t + 1)
                            else:
                                pe.wait_ge(S["k_diag_ready"], c[0] * 4 + t + 1)
                    for a in range(2):
                        last = pe.matmul(PAIR[t][:, a, 0:HPT // 2 * NK], qt[0][:, t, q * P:(q + 1) * P],
                                         k_diag[0][:, t, HPT // 2 * a:HPT // 2 * (a + 1), :],
                                         start=True, stop=True)
                    last.then_inc(S["s_ps"], 1)

            def turn_max(c):
                pe.wait_ge(S["max_ready"], upto(c, QT * KT, QT * KT))
                for q in range(QT):
                    last = pe.transpose(TURNED[0][0:H, q * P:(q + 1) * P].bitcast(F32R), neg_max[:, q, :],
                                        ident[:])
                last.then_inc(S["mt_ps"], 1)

            for k in range(KT):
                turn_x(FIRST, TURNED, k)
            pe.wait_ge(S["ctx_t_ready"], KT)
            pe.wait_ge(S["wkv_loaded"], 16)
            for t in range(KT):
                for k in range(KT):
                    last = pe.matmul(BANK[CD[t]][:, 0:B * NK], wkv_raw[:, k, t * P:(t + 1) * P], ctx_t[:, k, :],
                                     start=(k == 0), stop=(k == KT - 1))
                last.then_inc(S["kd_ps"], 1)
            pe.wait_ge(S["wq_loaded"], 16)
            pe.wait_ge(S["par_loaded"], 16)
            for t in range(KT):
                for k in range(KT):
                    last = pe.matmul(BANK["A"][:, t:t + 1], wq_raw[:, k, t * P:(t + 1) * P],
                                     par[:, BQ + k:BQ + k + 1], start=(k == 0), stop=(k == KT - 1))
            last.then_inc(S["qb_ps"], 1)
            pe.wait_ge(S["wq_lo_ready"], KT)
            project_q(FIRST, PROJ)
            pe.wait_ge(S["kd_lo_ready"], KT)
            for k in range(KT):
                turn_x(SECOND, CD_BANKS, k)
            pe.wait_ge(S["qb_ready"], 1)

            def project_v(b):
                if b >= 2:
                    pe.wait_ge(S["v_ready"], b - 1)
                for k in range(KT):
                    last = pe.matmul(BANK[AB[b % 2]][0:NK, 0:D], ctx_t[:, k, b * NK:(b + 1) * NK],
                                     wkv_raw[:, k, D:2 * D], start=(k == 0), stop=(k == KT - 1))
                last.then_inc(S["vd_ps"], 1)

            for q in range(QT):
                scores(FIRST, q, True)
                if q in (1, 2):
                    project_v(q - 1)
            turn_max(FIRST)
            project_v(2)
            project_v(3)
            project_q(SECOND, CD_BANKS)

            def up_tile(c, f):
                if f == 0:
                    pe.wait_ge(S["x2_lo_ready"], upto(c, KT, KT))
                    if first(c):
                        pe.wait_ge(S["w1_lo_ready"], 1)
                        pe.wait_ge(S["q_lo_ready"], upto(SECOND, KT, KT))
                if f >= 2:
                    pe.wait_ge(S["h_full_ready"], upto(c, FT, f - 1))
                elif not first(c):
                    pe.wait_ge(S["y_ready"], upto(step(c, -1), 2, f + 1))
                for n, (w, a) in enumerate(SPLITS):
                    for k in range(KT):
                        last = pe.matmul(BANK[CD[f % 2]], w1[w][:, k, f * P:(f + 1) * P], x2t[a][:, k, :],
                                         start=(n == 0 and k == 0), stop=(n == 2 and k == KT - 1))
                last.then_inc(S["h_ps"], 1)

            def values(core, j):
                if j == 0 and core[1] == 0:
                    pe.wait_ge(S["v_ones_ready"], core[0] + 1)
                if j == 0 and not first(core):
                    pe.wait_ge(S["x2_lo_ready"], upto(step(core, -1), KT, KT))
                if j >= 2:
                    pe.wait_ge(S["o_raw_ready"], upto(core, QT, j - 1))
                pe.wait_ge(S["exp_ready"], upto(core, NP, 2 * j + 2))
                for n in range(4):
                    last = pe.matmul(BANK[AB[j % 2]][32 * n:32 * n + 32, :],
                                     v_ones[:, 4 * j + n, :, :].rearrange("k e d -> k (e d)"),
                                     probs[0:NK, (2 * j + n // 2) % PTR, n % 2, :], start=True, stop=True,
                                     tile_position=(0, 32 * n))
                last.then_inc(S["pv_ps"], 1)

            def part1(core, down, nxt):
                def down_tile(f, halves=(0, 1)):
                    if down is None:
                        return
                    for s in halves:
                        if f == 0:
                            pe.wait_ge(S["h_full_ready"], upto(down, FT, FT if len(halves) == 2 else FT - 1 + s))
                            if first(down):
                                pe.wait_ge(S["w2_lo_ready"], 1)
                        if f % 2 == 0:
                            pe.wait_ge(S["h_lo_ready"], upto(down, FT // 2, f // 2 + 1))
                        for q in range(2):
                            for n, (a, w) in enumerate(SPLITS):
                                last = pe.matmul(BANK[CD[s]][:, q * D:(q + 1) * D],
                                                 h[a][:, f, (2 * s + q) * P:(2 * s + q + 1) * P], w2[w][:, f, :],
                                                 start=(f == 0 and q == 0 and n == 0), stop=(f == FT - 1 and n == 2),
                                                 skip_group_check=True)
                        if f == FT - 1:
                            last.then_inc(S["y_ps"], 1)

                if core is None:
                    for s in range(2):
                        for f in range(FT):
                            down_tile(f, (s,))
                    return
                down_tile(0)
                down_tile(1)
                down_tile(2)
                if second(core):
                    up_tile(FIRST, 0)
                    up_tile(FIRST, 1)
                down_beside = {0: 3, 1: 4, 2: 5, 4: 6, 6: 7}
                for g in range(NP):
                    if core is not None:
                        if g == 0:
                            pe.wait_ge(S["q_stack_loaded"], upto(core, Q_DMAS * 16, Q_DMAS * 16))
                            if first(core):
                                pe.wait_ge(S["pick_loaded"], 16)
                                pe.wait_ge(S["first_keys_by_pool"], 2 * QPT * 16)
                                pe.wait_ge(S["first_keys_by_sp"], QPT * 16)
                            elif core[1] == 0:
                                pe.wait_ge(S["k_stack_loaded"], core[0] * (K_DMAS * 16))
                        if g >= 2:
                            pe.wait_ge(S["exp_ready"], upto(core, NP, g - 1))
                        for e in range(2):
                            last = pe.matmul(PAIR[g % 2][0:NK, e, :], k_stack[:, 2 * g + e, :], q_stack[:, g, :],
                                             start=True, stop=True)
                        last.then_inc(S["st_ps"], 1)
                    if g in down_beside:
                        down_tile(down_beside[g])
                    if core is not None and g % 2 == 1 and g >= 3:
                        values(core, (g - 3) // 2)

            def part2(tail, front, up, new_batch):
                def up_beside(f):
                    if up is not None and not (first(up) and f < 2):
                        up_tile(up, f)

                def turn_o(*qs):
                    if tail is None:
                        return
                    for q in qs:
                        if q == 0:
                            pe.wait_ge(S["o_raw_ready"], upto(tail, QT, QT))
                        if q >= 2:
                            pe.wait_ge(S["o_nat_ready"], upto(tail, QT, q - 1))
                        for j in range(QT):
                            last = turn(BANK[AB[q % 2]][:, j * P:(j + 1) * P], o_raw[:, j, q * P:(q + 1) * P])
                        last.then_inc(S["ot_ps"], 1)

                def scores_at(place):
                    for q in maxima_at(front, place):
                        scores(front, q, new_batch)

                turned = front is None or second(front)
                if not turned:
                    pe.wait_ge(S["exp_ready"], upto(tail, NP, NP - 1))
                    turn_x(front, TURNED, 0)
                if tail is not None:
                    values(tail, 3)
                if not turned:
                    pe.wait_ge(S["exp_ready"], upto(tail, NP, NP))
                    turn_x(front, TURNED, 1)
                up_beside(0)
                scores_at("start")
                turn_o(0, 1)
                up_beside(1)
                scores_at("half divided")
                turn_o(2, 3)
                scores_at("divided")
                if not turned:
                    project_q(front, PROJ)
                up_beside(2)
                if tail is not None:
                    pe.wait_ge(S["o_nat_ready"], upto(tail, QT, QT))
                    for k in range(KT):
                        for q in range(QT):
                            last = turn(BANK[AB[k]][:, q * P:(q + 1) * P], o_nat[:, q, k * P:(k + 1) * P])
                        last.then_inc(S["at_ps"], 1)
                up_beside(3)
                scores_at("turned")
                if front is None:
                    up_beside(4)
                if tail is not None:
                    if first(tail):
                        pe.wait_ge(S["wo_lo_ready"], 1)
                    pe.wait_ge(S["o_lo_ready"], upto(tail, KT, KT))
                    for s in range(2):
                        for q in range(2):
                            m = 0
                            for a, w in SPLITS:
                                for k in range(KT):
                                    last = pe.matmul(BANK[AB[s]][:, q * D:(q + 1) * D],
                                                     xt[a][:, k, (2 * s + q) * P:(2 * s + q + 1) * P], wo[w][:, k, :],
                                                     start=(m == 0), stop=(m == 3 * KT - 1))
                                    m += 1
                        last.then_inc(S["op_ps"], 1)
                if front is not None:
                    up_beside(4)
                scores_at("projected")
                up_beside(5)
                scores_at("residual")
                up_beside(6)
                scores_at("end")
                up_beside(7)
                if front is not None:
                    turn_max(front)
                if tail is not None:
                    pe.wait_ge(S["x2_ready"], upto(tail, 2, 2))
                    _, u = tail
                    for k in range(KT):
                        for q in range(QT):
                            last = turn(BANK[AB[k]][:, q * P:(q + 1) * P], x2[u][:, q, k * P:(k + 1) * P])
                        last.then_inc(S["x2t_ps"], 1)

            phases(pe, part1, part2)


def kernel(**inputs):
    import numpy as np
    import concourse.bacc as bacc
    from concourse.bass_utils import run_bass_kernel_spmd as run

    a = {k.replace("L0_xattn_", ""): np.asarray(v) for k, v in inputs.items()}

    def by_rows(w):
        return np.ascontiguousarray(w.T.reshape(-1, P, w.shape[0]).transpose(1, 0, 2))

    def columns(v):
        return v.reshape(-1, P).T

    arrays = {
        "x": a["x"], "ctx": a["ctx_1024"],
        "wqT": by_rows(a["Wq"]), "wkvT": by_rows(a["Wkv"]), "woT": by_rows(a["Wo"]),
        "w1T": by_rows(a["W1"]), "w2T": by_rows(a["W2"]),
        "params": np.concatenate([columns(a[n]) for n in ("ln_q_g", "ln_q_b", "ln_kv_g", "ln_kv_b", "b1")], axis=1),
        "bo": np.broadcast_to(a["bo"], (P, D)), "b2": np.broadcast_to(a["b2"], (P, D)),
    }
    arrays = {f"in_{k}": np.ascontiguousarray(v) for k, v in arrays.items()}
    nc = bacc.Bacc("TRN2", target_bir_lowering=False, num_devices=1)
    args = [nc.dram_tensor(k, v.shape, mybir.dt.from_np(v.dtype), kind="ExternalInput").ap()
            for k, v in arrays.items()]
    out = nc.dram_tensor("out", (B, NQ, D), F32, kind="ExternalOutput").ap()
    build(nc, *args, out)
    r = run(nc, [arrays], core_ids=[0])
    return r.results[0]["out"]
```
